# Optimizing a Trainium2 kernel written in Bass

```python
import numpy as np
import jax
import jax.numpy as jnp

def _softmax(x, axis=-1):
    return jax.nn.softmax(x, axis=axis)

def _gelu(x):
    return jax.nn.gelu(x, approximate=True)

def _silu(x):
    return jax.nn.silu(x)

def _sigmoid(x):
    return jax.nn.sigmoid(x)

def _layernorm(x, axis=-1, eps=1e-05):
    m = jnp.mean(x, axis=axis, keepdims=True)
    v = jnp.var(x, axis=axis, keepdims=True)
    return (x - m) / jnp.sqrt(v + eps)

def _scatter_add(tgt, idx, src, axis=0):
    return tgt.at[idx].add(src)

def _segment_sum(src, seg, n):
    return jax.ops.segment_sum(src, seg, n)
kernel_name = 'mk_xattn_ffn_d1_seqx_r2_ccf6ff'

def setup_inputs(seed: int=0):
    np.random.seed(seed)
    _w = jnp.asarray

    def _rec_inputs():
        import jax
        import jax.numpy as jnp
        _rk = jax.random.key(seed)
        x = 0.0001212 + 1 * jax.random.normal(jax.random.fold_in(_rk, 1), (4, 1024, 1024), jnp.float32)
        _lenS = 1024 - jax.random.randint(jax.random.fold_in(_rk, 7), (4,), 0, max(1, 1024 // 4) + 1, jnp.int32)
        _lenS2 = 1024 - jax.random.randint(jax.random.fold_in(_rk, 8), (4,), 0, max(1, 1024 // 4) + 1, jnp.int32)
        _ctx_2048P = jax.random.normal(jax.random.fold_in(_rk, 11), (4, 16, 1024), jnp.float32)
        _ctx_2048c = jax.random.dirichlet(jax.random.fold_in(_rk, 511), 0.3 * jnp.ones((16,), jnp.float32), (4, 1024))
        _ctx_2048t = jnp.einsum('bsk,bkd->bsd', _ctx_2048c, _ctx_2048P)
        _ctx_2048t = _ctx_2048t * jax.lax.rsqrt(jnp.mean(jnp.square(_ctx_2048t)) + 1e-12) * 0.953939
        ctx_2048 = 0.000173663 + 1.0001 * (_ctx_2048t + 0.3 * jax.random.normal(jax.random.fold_in(_rk, 611), (4, 1024, 1024), jnp.float32))
        return (x, ctx_2048)
    x, ctx_2048 = _rec_inputs()

    def _L0_xattn_setup():
        import jax, jax.numpy as jnp
        import numpy as np
        B_DIM, T_DIM, C_DIM = (16, 512, 1024)

        def _wkv(w, u, k, v):
            Bn, Tn, Cn = k.shape
            NEG_INF = jnp.float32(-1e+38)

            def step(carry, kv_t):
                p, q, o = carry
                kt, vt = kv_t
                no = jnp.maximum(o, u + kt)
                A = jnp.exp(o - no)
                E = jnp.exp(u + kt - no)
                y = (A * p + E * vt) / (A * q + E)
                no2 = jnp.maximum(w + o, kt)
                A2 = jnp.exp(w + o - no2)
                E2 = jnp.exp(kt - no2)
                return ((A2 * p + E2 * vt, A2 * q + E2, no2), y)
            init = (jnp.zeros((Bn, Cn), k.dtype), jnp.zeros((Bn, Cn), k.dtype), jnp.full((Bn, Cn), NEG_INF, k.dtype))
            kT = jnp.moveaxis(k, 1, 0)
            vT = jnp.moveaxis(v, 1, 0)
            _, yT = jax.lax.scan(step, init, (kT, vT))
            return jnp.moveaxis(yT, 0, 1)
        key = jax.random.key(seed)
        k1, k2, k3, k4 = jax.random.split(key, 4)
        w = -jnp.exp(jax.random.normal(k1, (C_DIM,), jnp.float32))
        u = jax.random.normal(k2, (C_DIM,), jnp.float32)
        k = jax.random.normal(k3, (B_DIM, T_DIM, C_DIM), jnp.float32)
        v = jax.random.normal(k4, (B_DIM, T_DIM, C_DIM), jnp.float32)
        return {'B': B_DIM, 'T': T_DIM, 'C': C_DIM, 'w': w, 'u': u, 'k': k, 'v': v}
    _L0_xattn_all = _L0_xattn_setup()
    _L0_xattn_in = {k: v for k, v in _L0_xattn_all.items() if k in ('w', 'u')}
    del _L0_xattn_all

    def _L0_ffn_setup():
        import jax, jax.numpy as jnp
        import numpy as np
        B, S, D, E, FF, TOPK = (4, 1024, 1024, 8, 256, 2)
        key = jax.random.key(seed)
        k0, k1, k2, k3, k4 = jax.random.split(key, 5)
        x = jax.random.normal(k0, (B, S, D), dtype=jnp.float32)
        router_w = jax.random.normal(k1, (E, D), dtype=jnp.float32) * 0.02
        w1 = jax.random.normal(k2, (E, D, FF), dtype=jnp.float32) * 0.02
        w2 = jax.random.normal(k3, (E, FF, D), dtype=jnp.float32) * 0.02
        w3 = jax.random.normal(k4, (E, D, FF), dtype=jnp.float32) * 0.02
        return {'x': x, 'router_w': router_w, 'w1': w1, 'w2': w2, 'w3': w3}
    _L0_ffn_all = _L0_ffn_setup()
    _L0_ffn_in = {k: v for k, v in _L0_ffn_all.items() if k in ('router_w', 'w1', 'w2', 'w3')}
    del _L0_ffn_all
    return {'x': x, 'ctx_2048': ctx_2048, 'L0_xattn_w': _L0_xattn_in['w'], 'L0_xattn_u': _L0_xattn_in['u'], 'L0_ffn_router_w': _L0_ffn_in['router_w'], 'L0_ffn_w1': _L0_ffn_in['w1'], 'L0_ffn_w2': _L0_ffn_in['w2'], 'L0_ffn_w3': _L0_ffn_in['w3']}

def reference(x, ctx_2048, L0_xattn_w, L0_xattn_u, L0_ffn_router_w, L0_ffn_w1, L0_ffn_w2, L0_ffn_w3):
    import jax
    import jax.numpy as jnp

    def _L0_xattn_ref(B, T, C, w, u, k, v):
        import jax, jax.numpy as jnp
        import numpy as np
        B_DIM, T_DIM, C_DIM = (16, 512, 1024)

        def _wkv(w, u, k, v):
            Bn, Tn, Cn = k.shape
            NEG_INF = jnp.float32(-1e+38)

            def step(carry, kv_t):
                p, q, o = carry
                kt, vt = kv_t
                no = jnp.maximum(o, u + kt)
                A = jnp.exp(o - no)
                E = jnp.exp(u + kt - no)
                y = (A * p + E * vt) / (A * q + E)
                no2 = jnp.maximum(w + o, kt)
                A2 = jnp.exp(w + o - no2)
                E2 = jnp.exp(kt - no2)
                return ((A2 * p + E2 * vt, A2 * q + E2, no2), y)
            init = (jnp.zeros((Bn, Cn), k.dtype), jnp.zeros((Bn, Cn), k.dtype), jnp.full((Bn, Cn), NEG_INF, k.dtype))
            kT = jnp.moveaxis(k, 1, 0)
            vT = jnp.moveaxis(v, 1, 0)
            _, yT = jax.lax.scan(step, init, (kT, vT))
            return jnp.moveaxis(yT, 0, 1)
        return _wkv(w, u, k, v)

    def _L0_ffn_ref(x, router_w, w1, w2, w3):
        import jax, jax.numpy as jnp
        import numpy as np
        B, S, D, E, FF, TOPK = (4, 1024, 1024, 8, 256, 2)
        bsz, seq, dim = x.shape
        num_experts = router_w.shape[0]
        x_flat = x.reshape(-1, dim)
        expert_scores = x_flat @ router_w.T
        top_scores, selected = jax.lax.top_k(expert_scores, TOPK)
        top_scores = jax.nn.softmax(top_scores.astype(jnp.float32), axis=-1).astype(x.dtype)
        flat_expert_idx = selected.reshape(-1)
        num_tokens_per_expert = jnp.bincount(flat_expert_idx, length=num_experts)
        sorted_indices = jnp.argsort(flat_expert_idx, stable=True)
        scatter_indices = sorted_indices // TOPK
        x_gathered = x_flat[scatter_indices]
        scores_sorted = top_scores.reshape(-1)[sorted_indices]
        xb = x_gathered.astype(jnp.bfloat16)
        gs = num_tokens_per_expert.astype(jnp.int32)
        w1b = w1.astype(jnp.bfloat16)
        w2b = w2.astype(jnp.bfloat16)
        w3b = w3.astype(jnp.bfloat16)
        x1 = jax.lax.ragged_dot(xb, w1b, gs)
        x3 = jax.lax.ragged_dot(xb, w3b, gs)
        h = jax.nn.silu(x1) * x3
        routed = jax.lax.ragged_dot(h, w2b, gs).astype(x.dtype)
        weighted = routed * scores_sorted[:, None]
        out_flat = jnp.zeros_like(x_flat).at[scatter_indices].add(weighted)
        return out_flat.reshape(bsz, seq, dim)
    x = x + _L0_xattn_ref(4, 1024, 1024, L0_xattn_w, L0_xattn_u, _layernorm(x, axis=-1), ctx_2048)
    x = x + _L0_ffn_ref(_layernorm(x, axis=-1), L0_ffn_router_w, L0_ffn_w1, L0_ffn_w2, L0_ffn_w3)
    return x

_drawn_inputs = setup_inputs


def setup_inputs(seed=0):
    import zlib

    import numpy as np

    out = dict(_drawn_inputs(seed))
    spreads = {}
    factors = {}
    for name, (base, spread) in spreads.items():
        noise = np.random.default_rng([zlib.crc32(name.encode()), seed]).standard_normal(out[name].shape)
        drawn = base * np.exp(spread * noise) if base else spread * noise
        out[name] = jnp.asarray(drawn.astype(out[name].dtype))
    for name, factor in factors.items():
        out[name] = (out[name] * factor).astype(out[name].dtype)
    return out
```

```python
from contextlib import ExitStack

import concourse.bass as bass
from concourse import mybir

ALU = mybir.AluOpType
ACT = mybir.ActivationFunctionType
AX_X = mybir.AxisListType.X
F32 = mybir.dt.float32
BF16 = mybir.dt.bfloat16
I32 = mybir.dt.int32
U32 = mybir.dt.uint32

P = 128
EPS = 1e-5
U_CAP = 50.0
DMA = 16


class Signal:

    def __init__(self, handle):
        self.handle, self.count = handle, 0


class Streams:

    def __init__(self, engines):
        self.lists = {e: [] for e in engines}
        self.passed = {}

    def put(self, engine, instruction, signal=None, by=1):
        self.lists[engine].append((instruction, signal, by))
        if signal is None:
            return None
        signal.count += by
        return signal, signal.count

    def wait(self, engine, *marks):
        for mark in marks:
            if mark is None:
                continue
            signal, value = mark
            if self.passed.get((engine, signal), 0) < value:
                self.passed[engine, signal] = value
                self.lists[engine].append((None, signal, value))

    def emit(self, name, engine):
        for instruction, signal, number in self.lists[name]:
            if instruction is None:
                engine.wait_ge(signal.handle, number)
                continue
            made = instruction(engine)
            if signal is not None:
                made.then_inc(signal.handle, number)


def wkv_moe(nc, x, ctx, decay, bonus, router, w1, w2, w3, out):
    B, T, D = x.shape
    E, _, FF = w1.shape
    TOPK = 2
    TOKENS = B * T
    UNIT = 512
    UT = UNIT // P
    UNITS = TOKENS // UNIT
    PER_ROW = T // UNIT
    J = D // P
    GROUPS = 2
    GT = TOKENS // GROUPS
    GTILES = GT // P
    GUNITS = UNITS // GROUPS
    SPARE = E - 1
    KT = GT * TOPK // P + SPARE
    REGION = GT // P + 1
    GREG = E * REGION + SPARE
    FC = FF // P
    R1 = E + 1

    x_rows = x.rearrange("b t d -> (b t) d")
    ctx_rows = ctx.rearrange("b t d -> (b t) d")
    out_rows = out.rearrange("b t d -> (b t) d")
    sorted_x = nc.dram_tensor("sorted_x", [GROUPS * GREG * P, D], BF16, kind="Internal").ap()
    expert_y = [nc.dram_tensor(f"expert_y{g}", [KT * P, D], BF16, kind="Internal").ap() for g in range(GROUPS)]
    residual = nc.dram_tensor("residual", [TOKENS, D], F32, kind="Internal").ap()

    with ExitStack() as stack:
        def sb(name, shape, dt):
            return stack.enter_context(nc.sbuf_tensor(name, shape, dt))

        def sig(name):
            return Signal(stack.enter_context(nc.semaphore(name)))

        w13_sb = sb("w13_sb", [P, E * J * 2 * FF], BF16)
        w2_sb = sb("w2_sb", [P, E * FC * D], BF16)
        XSLOTS, VSLOTS, NSLOTS = 2 * UT, 2, 4
        x_sb = sb("x_sb", [P, XSLOTS, D], F32)
        v_sb = sb("v_sb", [P, VSLOTS, D], F32)
        ek_odd = sb("ek_odd", [P, 2 * UT * D], F32)
        scan_sb = sb("scan_sb", [P, 2, 2, UNIT + 1], F32)
        ND = 3
        num_sb = sb("num_sb", [P, ND, UNIT], F32)
        den_sb = sb("den_sb", [P, ND, UNIT], F32)
        x1t_sb = sb("x1t_sb", [P, 2, UNIT], F32)
        xn_sb = sb("xn_sb", [P, NSLOTS, D], BF16)
        ek_even = w2_sb[:, :].bitcast(F32)
        ek_all = [b.rearrange("p (s i d) -> p s i d", s=2, i=UT) for b in (ek_even, ek_odd[:, :])]

        ident = sb("ident", [P, P], F32)
        ident_b = sb("ident_b", [P, P], BF16)
        before_b = sb("before_b", [P, P], BF16)
        ones_b = sb("ones_b", [P, P], BF16)
        eps_sb = sb("eps_sb", [P, 1], F32)
        router_t = sb("router_t", [P, J, R1], F32)
        router_sum = sb("router_sum", [P, E], F32)
        chan = sb("chan", [P, 2, J], F32)
        chan_k = sb("chan_k", [P, 4, J], F32)
        state = sb("state", [P, J, 2], F32)
        stats = sb("stats", [P, 2, 12], F32)
        mv = sb("mv", [P, XSLOTS, 2], F32)
        norm1 = sb("norm1", [P, XSLOTS, 3], F32)
        sc_sb = sb("sc_sb", [P, UT, R1], F32)
        negmean = sb("negmean", [P, UT], F32)
        sumsq = sb("sumsq", [P, UT], F32)
        norm2 = sb("norm2", [P, 3, UT], F32)
        score = sb("score", [P, UT, E], F32)
        top = sb("top", [P, UT, 8], F32)
        top_i = sb("top_i", [P, UT, 8], U32)
        top_f = sb("top_f", [P, TOPK, UT], F32)
        chosen = sb("chosen", [P, TOPK, UT, E], F32)
        mask_b = sb("mask_b", [P, UT, E], BF16)
        before_cnt = sb("before_cnt", [P, GTILES + 1, E], BF16)
        gap = sb("gap", [P, 3, UT], F32)
        place = sb("place", [P, UT, E], F32)
        picked = sb("picked", [P, TOPK, UT, E], F32)
        place_f = sb("place_f", [P, TOPK, UT], F32)
        iota_e = sb("iota_e", [P, E], F32)
        iota_p = sb("iota_p", [P, E], F32)
        weight_sb = sb("weight_sb", [P, TOKENS // P, TOPK], F32)
        place_i = sb("place_i", [P, TOKENS // P, TOPK], I32)
        expert_sb = sb("expert_sb", [P, TOKENS // P, TOPK], F32)
        pad_f = sb("pad_f", [P, E], F32)
        pad_i = sb("pad_i", [P, GROUPS, E], I32)
        cnt_sb = sb("cnt_sb", [P, GROUPS, E], F32)
        table_i = sb("table_i", [P, GROUPS, 2, KT], I32)

        XS, YB, CB = 8, 4, 4
        ek_b = ek_odd[:, :].bitcast(BF16)
        xs_sb = ek_b[:, 0:XS * D].rearrange("p (s c t) -> p s c t", s=XS, c=J)
        y_sb = ek_b[:, XS * D:(XS + YB) * D].rearrange("p (s d) -> p s d", s=YB)
        num_b = num_sb[:, :, :].rearrange("p a b -> p (a b)").bitcast(BF16)
        silu_sb = num_b[:, 0:2 * FF].rearrange("p (s f) -> p s f", s=2)
        h_sb = num_b[:, 2 * FF:4 * FF].rearrange("p (s f) -> p s f", s=2)
        ht_sb = num_b[:, 4 * FF:6 * FF].rearrange("p (s f) -> p s f", s=2)
        v_b = v_sb[:, :, :].rearrange("p a b -> p (a b)").bitcast(BF16)
        pick_sb = v_b.rearrange("p (s d) -> p s d", d=D)
        tab = den_sb[:, :, :].rearrange("p a b -> p (a b)")

        bank = [stack.enter_context(nc.psum_tensor(f"bank{i}", [P, 512], F32)) for i in range(8)]
        ps_e, ps_v, ps_x, ps_b, ps_score, ps_small = bank[0], bank[1], bank[2:4], bank[4:6], bank[6], bank[7]

        s_const, s_setup_dma, s_setup_pe, s_setup_dve, s_setup_act = map(
            sig, ("s_const", "s_setup_dma", "s_setup_pe", "s_setup_dve", "s_setup_act"))
        s_x = [sig(f"s_x_in{i}") for i in range(XSLOTS)]
        s_v = [sig(f"s_v_in{i}") for i in range(VSLOTS)]
        s_spill = [sig(f"s_spill{i}") for i in range(2)]
        s_stats, s_norm1, s_nmr1, s_exp, s_ev = map(sig, ("s_stats", "s_norm1", "s_nmr1", "s_exp", "s_ev"))
        s_te, s_tv, s_tx, s_router, s_back = map(sig, ("s_te", "s_tv", "s_tx", "s_router", "s_back"))
        s_scan, s_den, s_num, s_log, s_inv, s_y, s_x1t, s_x1 = map(
            sig, ("s_scan", "s_den", "s_num", "s_log", "s_inv", "s_y", "s_x1t", "s_x1"))
        s_carry = sig("s_carry")
        s_route, s_norm2, s_nmr2, s_soft, s_xn, s_rank = map(
            sig, ("s_route", "s_norm2", "s_nmr2", "s_soft", "s_xn", "s_rank"))
        s_scatter = [sig(f"s_scatter{i}") for i in range(NSLOTS)]
        s_pad, s_zero, s_w13 = sig("s_pad"), sig("s_zero"), sig("s_w13")
        s_w2 = sig("s_w2")
        s_table, s_total = sig("s_table"), sig("s_total")
        s_xs = [sig(f"s_xs{i}") for i in range(XS)]
        s_h, s_silu, s_gate, s_ht, s_htc, s_yp, s_ya, s_yd = map(
            sig, ("s_h", "s_silu", "s_gate", "s_ht", "s_htc", "s_yp", "s_ya", "s_yd"))
        s_yout = [sig(f"s_yout{i}") for i in range(YB)]
        s_res = [sig(f"s_res{i}") for i in range(CB)]
        s_pick = [sig(f"s_pick{i}") for i in range(2)]
        s_out = [sig(f"s_out{i}") for i in range(CB)]
        s_sum = sig("s_sum")

        S = Streams(("sync", "gpsimd", "scalar", "vector", "tensor"))
        put, wait = S.put, S.wait

        def diagonal(tile, compare, fill):
            made = put("gpsimd", lambda g: g.memset(tile[:, :], 1.0 - fill), s_const)
            wait("gpsimd", made)
            return put("gpsimd", lambda g: g.affine_select(
                out=tile[:, :], in_=tile[:, :], compare_op=compare, fill=fill, base=0,
                pattern=[[-1, P]], channel_multiplier=1), s_const)

        put("gpsimd", lambda g: g.memset(xn_sb[:, 0, :], 0.0), s_const)
        put("gpsimd", lambda g: g.memset(eps_sb[:, :], EPS), s_const)
        put("gpsimd", lambda g: g.memset(ones_b[:, :], 1.0), s_const)
        put("gpsimd", lambda g: g.memset(router_t[:, :, E:R1], 1.0), s_const)
        put("gpsimd", lambda g: g.memset(before_cnt[:, 0, :], 0.0), s_const)
        ones_f = x1t_sb[:, 0, 0:P]
        put("gpsimd", lambda g: g.memset(ones_f, 1.0), s_const)
        put("gpsimd", lambda g: g.iota(iota_e[:, :], pattern=[[1, E]], base=0, channel_multiplier=0,
                                       allow_small_or_imprecise_dtypes=True), s_const)
        put("gpsimd", lambda g: g.iota(iota_p[:, :], pattern=[[REGION * P, E]], base=0, channel_multiplier=1,
                                       allow_small_or_imprecise_dtypes=True), s_const)
        diagonal(ident, ALU.not_equal, 1.0)
        diagonal(ident_b, ALU.not_equal, 1.0)
        made = put("gpsimd", lambda g: g.memset(before_b[:, :], 1.0), s_const)
        wait("gpsimd", made)
        const = put("gpsimd", lambda g: g.affine_select(
            out=before_b[:, :], in_=before_b[:, :], compare_op=ALU.is_gt, fill=0.0, base=0,
            pattern=[[1, P]], channel_multiplier=-1), s_const)

        rows = den_sb[0:2 * J, 0, 0:P]
        router_rows = num_sb[0:E, 0:2, :].rearrange("p a b -> p (a b)")
        put("scalar", lambda a: a.dma_start(den_sb[0:J, 0, 0:P], decay.rearrange("(j p) -> j p", p=P)),
            s_setup_dma, DMA)
        put("scalar", lambda a: a.dma_start(den_sb[J:2 * J, 0, 0:P], bonus.rearrange("(j p) -> j p", p=P)),
            s_setup_dma, DMA)
        small_in = put("scalar", lambda a: a.dma_start(router_rows, router[:, :]), s_setup_dma, DMA)
        wait("tensor", const, small_in)
        for j in range(J):
            put("tensor", lambda t, j=j: t.transpose(ps_small[:, j * E:(j + 1) * E],
                                                     router_rows[:, j * P:(j + 1) * P], ident[0:E, 0:E]))
        turned = put("tensor", lambda t: t.transpose(ps_b[0][:, 0:2 * J], rows, ident[0:2 * J, 0:2 * J]),
                     s_setup_pe)
        wait("vector", const, turned)
        router_in = put("vector", lambda v: v.tensor_copy(
            router_t[:, :, 0:E], ps_small[:, 0:J * E].rearrange("p (j e) -> p j e", j=J)), s_setup_dve)
        put("vector", lambda v: v.tensor_copy(
            chan[:, :, :], ps_b[0][:, 0:2 * J].rearrange("p (s j) -> p s j", s=2)), s_setup_dve)
        wait("vector", (s_setup_dve, s_setup_dve.count))
        put("vector", lambda v: v.tensor_scalar(chan_k[:, 2, :], chan[:, 1, :], 0.0, -1.0, ALU.max, ALU.mult),
            s_setup_dve)
        chan_in = put("vector", lambda v: v.tensor_scalar(chan_k[:, 1, :], chan[:, 1, :], U_CAP, None, ALU.min),
                      s_setup_dve)
        put("scalar", lambda a: a.preload_act_table_set("natural_log_exp_and_others"))
        wait("scalar", chan_in)
        put("scalar", lambda a: a.activation(chan_k[:, 0, :], chan[:, 0, :], ACT.Exp), s_setup_act)
        put("scalar", lambda a: a.activation(chan_k[:, 1, :], chan_k[:, 1, :], ACT.Exp), s_setup_act)
        chan_ready = put("scalar", lambda a: a.activation(chan_k[:, 3, :], chan_k[:, 2, :], ACT.Exp), s_setup_act)
        decay_k, bonus_k, shift_k, scale_k = (chan_k[:, n, :] for n in range(4))
        wait("tensor", router_in)
        for j in range(J):
            summed = put("tensor", lambda t, j=j: t.matmul(ps_small[:, 0:E], ones_f, router_t[:, j, 0:E],
                                                           start=(j == 0), stop=(j == J - 1)),
                         s_setup_pe if j == J - 1 else None)
        wait("vector", summed)
        router_summed = put("vector", lambda v: v.tensor_copy(router_sum[:, :], ps_small[:, 0:E]), s_setup_dve)
        wait("vector", chan_ready)

        wait("sync", const)
        for g in range(GROUPS):
            for t in range(SPARE):
                row = (g * GREG + E * REGION + t) * P
                zeroed = put("sync", lambda s, row=row: s.dma_start(sorted_x[row:row + P, :], xn_sb[:, 0, :]),
                             s_zero, DMA)
        w13 = w13_sb[:, :].rearrange("p (e c f) -> p e c f", e=E, c=J)
        w2v = w2_sb[:, :].rearrange("p (e c d) -> p e c d", e=E, c=FC)

        def load_w13(e):
            for part, w in enumerate((w1, w3)):
                mark = put("gpsimd", lambda g, e=e, part=part, w=w: g.dma_start(
                    w13[:, e, :, part * FF:(part + 1) * FF], w[e].rearrange("(c p) f -> p c f", p=P)), s_w13, DMA)
            return mark

        def load_w2(e):
            return put("gpsimd", lambda g, e=e: g.dma_start(
                w2v[:, e, :, :], w2[e].rearrange("(c p) d -> p c d", p=P)), s_w2, DMA)

        x_in, v_in, stat, nrm, nmr, e_in, ev_in = {}, {}, {}, {}, {}, {}, {}
        te, tv, tx, den, num, inv, ym, x1t, x1m, routed_pe = {}, {}, {}, {}, {}, {}, {}, {}, {}, {}
        carried, saved, spilled, squared, xn_m, scattered = {}, {}, {}, {}, {}, {}

        def load_tile(t):
            u = t // UT
            wait("sync", spilled.get(u - 2), squared.get(t - XSLOTS), xn_m.get(t - XSLOTS))
            x_in[t] = put("sync", lambda s, t=t: s.dma_start(x_sb[:, t % XSLOTS, :], x_rows[t * P:(t + 1) * P, :]),
                          s_x[t % XSLOTS], DMA)

        def load_ctx(t):
            wait("sync", ev_in.get(t - VSLOTS))
            v_in[t] = put("sync", lambda s, t=t: s.dma_start(v_sb[:, t % VSLOTS, :], ctx_rows[t * P:(t + 1) * P, :]),
                          s_v[t % VSLOTS], DMA)

        def first_norm(t):
            k = t % XSLOTS
            wait("vector", x_in[t], nmr.get(t - XSLOTS), nrm.get(t - XSLOTS))
            for h in range(2):
                mark = put("vector", lambda v, h=h: v.bn_stats(stats[:, t % 2, 6 * h:6 * h + 6],
                                                               x_sb[:, k, h * 512:(h + 1) * 512]), s_stats)
            wait("vector", mark)
            stat[t] = put("vector", lambda v: v.bn_aggr(mv[:, k, :], stats[:, t % 2, :]), s_stats)
            wait("scalar", stat[t], const, nmr.get(t - XSLOTS))
            mark = put("scalar", lambda a: a.activation(norm1[:, k, 0:1], mv[:, k, 1:2], ACT.Ln,
                                                        bias=eps_sb[:, 0:1]), s_norm1)
            wait("scalar", mark)
            nrm[t] = put("scalar", lambda a: a.activation(norm1[:, k, 1:2], norm1[:, k, 0:1], ACT.Exp,
                                                          scale=-0.5), s_norm1)
            wait("gpsimd", nrm[t], e_in.get(t - XSLOTS))
            nmr[t] = put("gpsimd", lambda g: g.tensor_scalar(norm1[:, k, 2:3], mv[:, k, 0:1], norm1[:, k, 1:2],
                                                             -1.0, ALU.mult, ALU.mult), s_nmr1)

        def exponentials(t):
            u, i, k = t // UT, t % UT, t % XSLOTS
            buf = ek_all[u % 2]
            wait("scalar", nmr[t], tv.get((u - 2) * J + J - 1))
            if u < 2 and u % 2 == 0:
                pass
            e_in[t] = put("scalar", lambda a: a.activation(buf[:, 0, i, :], x_sb[:, k, :], ACT.Exp,
                                                           bias=norm1[:, k, 2:3], scale=norm1[:, k, 1:2]), s_exp)
            wait("gpsimd", e_in[t], v_in[t])
            ev_in[t] = put("gpsimd", lambda g: g.tensor_tensor(buf[:, 1, i, :], buf[:, 0, i, :],
                                                               v_sb[:, t % VSLOTS, :], ALU.mult), s_ev)

        def turn(n):
            u, j = divmod(n, J)
            buf = ek_all[u % 2]
            for part, (dst, marks, free, done, s) in enumerate((
                    (ps_e, e_in, den.get(n - 1), te, s_te), (ps_v, ev_in, num.get(n - 1), tv, s_tv))):
                wait("tensor", const, marks[u * UT + UT - 1], free)
                for i in range(UT):
                    done[n] = put("tensor", lambda t, i=i, dst=dst, part=part: t.transpose(
                        dst[:, i * P:(i + 1) * P], buf[:, part, i, j * P:(j + 1) * P], ident[:, :]),
                        s if i == UT - 1 else None)

        def turn_x(n):
            u, j = divmod(n, J)
            wait("tensor", x1t.get(n - 2))
            for i in range(UT):
                tx[n] = put("tensor", lambda t, i=i: t.transpose(
                    ps_x[n % 2][:, i * P:(i + 1) * P], x_sb[:, (u * UT + i) % XSLOTS, j * P:(j + 1) * P],
                    ident[:, :]), s_tx if i == UT - 1 else None)

        def recur(n):
            u, j = divmod(n, J)
            first = u % PER_ROW == 0
            sums = scan_sb[:, n % 2, :, :]
            if not first:
                wait("gpsimd", num.get(n - 2), saved[n - J])
                carried[n] = put("gpsimd", lambda g: g.tensor_copy(sums[:, :, 0:1], state[:, j, :].unsqueeze(2)),
                                 s_carry)
                wait("vector", carried[n])
            else:
                wait("vector", saved.get(n - 2))
            for part, (src, turned_m, dst, done, s, free) in enumerate((
                    (ps_e, te[n], den_sb, den, s_den, ym.get(n - ND)),
                    (ps_v, tv[n], num_sb, num, s_num, x1t.get(n - ND)))):
                wait("vector", turned_m)
                if first:
                    put("vector", lambda v, part=part, src=src: v.tensor_copy(sums[:, part, 0:1], src[:, 0:1]),
                        s_scan)
                mark = put("vector", lambda v, part=part, src=src: v.tensor_tensor_scan(
                    out=sums[:, part, 1:UNIT + 1], data0=decay_k[:, j:j + 1].to_broadcast([P, UNIT]),
                    data1=src[:, :], initial=0.0 if first else sums[:, part, 0:1],
                    op0=ALU.mult, op1=ALU.add), s_scan)
                wait("vector", mark, free)
                done[n] = put("vector", lambda v, part=part, src=src, dst=dst: v.scalar_tensor_tensor(
                    out=dst[:, n % ND, :], in0=src[:, :], scalar=bonus_k[:, j:j + 1],
                    in1=sums[:, part, 0:UNIT], op0=ALU.mult, op1=ALU.add), s)
            if first:
                wait("gpsimd", num[n])
                saved[n] = put("gpsimd", lambda g: g.tensor_copy(state[:, j, :].unsqueeze(2),
                                                                 sums[:, :, UNIT:UNIT + 1]), s_carry)

        def divide(n):
            j = n % J
            wait("scalar", den[n])
            mark = put("scalar", lambda a: a.activation(den_sb[:, n % ND, :], den_sb[:, n % ND, :], ACT.Ln,
                                                        scale=scale_k[:, j:j + 1]), s_log)
            wait("scalar", mark)
            inv[n] = put("scalar", lambda a: a.activation(den_sb[:, n % ND, :], den_sb[:, n % ND, :], ACT.Exp,
                                                          bias=shift_k[:, j:j + 1], scale=-1.0), s_inv)
            wait("gpsimd", inv[n], num[n])
            ym[n] = put("gpsimd", lambda g: g.tensor_tensor(num_sb[:, n % ND, :], num_sb[:, n % ND, :],
                                                            den_sb[:, n % ND, :], ALU.mult), s_y)

        def add_residual(n):
            wait("vector", tx[n], ym[n], routed_pe.get(n - 2), router_summed, summed)
            x1t[n] = put("vector", lambda v: v.tensor_tensor(x1t_sb[:, n % 2, :], ps_x[n % 2][:, :],
                                                             num_sb[:, n % ND, :], ALU.add), s_x1t)

        copied_scores = {}

        def turn_back(n):
            u, j = divmod(n, J)
            wait("tensor", x1t[n], x1m.get(n - 2))
            if j == 0:
                wait("tensor", copied_scores.get(u - 1))
            for i in range(UT):
                put("tensor", lambda t, i=i: t.matmul(
                    ps_score[:, i * R1:(i + 1) * R1], x1t_sb[:, n % 2, i * P:(i + 1) * P], router_t[:, j, :],
                    start=(j == 0 and i == 0), stop=(j == J - 1), skip_group_check=True))
            for i in range(UT):
                routed_pe[n] = put("tensor", lambda t, i=i: t.transpose(
                    ps_b[n % 2][:, i * P:(i + 1) * P], x1t_sb[:, n % 2, i * P:(i + 1) * P], ident[:, :]),
                    s_back if i == UT - 1 else None)

        def keep_x1(n):
            u, j = divmod(n, J)
            s0 = (u * UT) % XSLOTS
            wait("scalar", routed_pe[n])
            x1m[n] = put("scalar", lambda a: a.activation(
                x_sb[:, s0:s0 + UT, j * P:(j + 1) * P],
                ps_b[n % 2][:, :].rearrange("p (i c) -> p i c", i=UT), ACT.Copy), s_x1)

        route = {}

        def second_norm(u):
            s0 = (u * UT) % XSLOTS
            last = x1m[u * J + J - 1]
            wait("sync", last)
            spilled[u] = put("sync", lambda s: s.dma_start(
                residual[u * UNIT:(u + 1) * UNIT, :].rearrange("(i p) d -> p i d", p=P),
                x_sb[:, s0:s0 + UT, :]), s_spill[u % 2], DMA)
            wait("vector", routed_pe[u * J + J - 1], *route.get(("free", u - 1), ()))
            copied_scores[u] = put("vector", lambda v: v.tensor_copy(
                sc_sb[:, :, :], ps_score[:, 0:UT * R1].rearrange("p (i e) -> p i e", i=UT)), s_route)
            wait("vector", copied_scores[u])
            neg = put("vector", lambda v: v.tensor_scalar(negmean[:, :], sc_sb[:, :, E], -1.0 / D, None, ALU.mult),
                      s_route)
            wait("vector", neg)
            wait("scalar", last, neg)
            for i in range(UT):
                t = u * UT + i
                wait("scalar", *scattered.get(t - NSLOTS, ()))
                if t < NSLOTS:
                    wait("scalar", zeroed)
                squared[t] = put("scalar", lambda a, i=i, t=t: a.activation(
                    xn_sb[:, t % NSLOTS, :], x_sb[:, s0 + i, :], ACT.Square, bias=negmean[:, i:i + 1],
                    accum_out=sumsq[:, i:i + 1]), s_norm2)
            wait("scalar", squared[u * UT + UT - 1])
            mark = put("scalar", lambda a: a.activation(norm2[:, 0, :], sumsq[:, :], ACT.Ln, scale=1.0 / D,
                                                        bias=eps_sb[:, 0:1]), s_norm2)
            wait("scalar", mark)
            route["std", u] = put("scalar", lambda a: a.activation(norm2[:, 1, :], norm2[:, 0, :], ACT.Exp,
                                                                   scale=-0.5), s_norm2)
            for i in range(UT):
                mark = put("vector", lambda v, i=i: v.scalar_tensor_tensor(
                    out=score[:, i, :], in0=router_sum[:, :], scalar=negmean[:, i:i + 1],
                    in1=sc_sb[:, i, 0:E], op0=ALU.mult, op1=ALU.add), s_route)
            wait("vector", mark)
            for i in range(UT):
                mark = put("vector", lambda v, i=i: v.max(top[:, i, :], score[:, i, :]), s_route)
            wait("vector", mark)
            for i in range(UT):
                mark = put("vector", lambda v, i=i: v.max_index(top_i[:, i, :], top[:, i, :], score[:, i, :]),
                           s_route)
            wait("vector", mark)
            mark = put("vector", lambda v: v.tensor_copy(
                top_f[:, :, :], top_i[:, :, 0:TOPK].rearrange("p i k -> p k i")), s_route)
            wait("vector", mark)
            put("vector", lambda v: v.tensor_copy(
                expert_sb[:, u * UT:(u + 1) * UT, :], top_f[:, :, :].rearrange("p k i -> p i k")), s_route)
            for k in range(TOPK):
                mark = put("vector", lambda v, k=k: v.tensor_tensor(
                    chosen[:, k, :, :], iota_e[:, :].unsqueeze(1).to_broadcast([P, UT, E]),
                    top_f[:, k, :].unsqueeze(2).to_broadcast([P, UT, E]), ALU.is_equal), s_route)
            wait("vector", mark)
            mark = put("vector", lambda v: v.tensor_tensor(mask_b[:, :, :], chosen[:, 0, :, :], chosen[:, 1, :, :],
                                                           ALU.add), s_route)
            for i in range(UT):
                g = (u % GUNITS) * UT + i
                wait("vector", mark)
                if g == 0:
                    wait("vector", route.get(("total", u // GUNITS - 1)))
                    before = before_cnt[:, 0, :]
                mark = put("vector", lambda v, i=i, g=g: v.tensor_tensor(
                    before_cnt[:, g + 1, :], before_cnt[:, g, :], mask_b[:, i, :], ALU.add), s_route)
            route["mask", u] = mark

        def rank_tokens(u):
            wait("tensor", route["mask", u], route.get(("place", u - 1)), router_summed,
                 route.get(("counted", u // GUNITS - 1)))
            for i in range(UT):
                g = (u % GUNITS) * UT + i
                dst = ps_small[:, i * E:(i + 1) * E]
                put("tensor", lambda t, i=i, dst=dst: t.matmul(dst, before_b[:, :], mask_b[:, i, :],
                                                               start=True, stop=False, skip_group_check=True))
                route["rank", u] = put("tensor", lambda t, g=g, dst=dst: t.matmul(
                    dst, ones_b[:, :], before_cnt[:, g, :], start=False, stop=True, skip_group_check=True),
                    s_rank)

        def normed_rows(u):
            s0 = (u * UT) % XSLOTS
            wait("gpsimd", route["std", u])
            mark = put("gpsimd", lambda g: g.tensor_tensor(norm2[:, 2, :], negmean[:, :], norm2[:, 1, :], ALU.mult),
                       s_nmr2)
            wait("gpsimd", mark)
            for i in range(UT):
                t = u * UT + i
                wait("gpsimd", squared[t])
                xn_m[t] = put("gpsimd", lambda g, i=i, t=t: g.tensor_scalar(
                    xn_sb[:, t % NSLOTS, :], x_sb[:, s0 + i, :], norm2[:, 1, i:i + 1], norm2[:, 2, i:i + 1],
                    ALU.mult, ALU.add), s_xn)
            wait("vector", route["std", u])
            mark = put("vector", lambda v: v.tensor_tensor(gap[:, 0, :], top[:, :, 1], top[:, :, 0], ALU.subtract),
                       s_soft)
            wait("vector", mark)
            mark = put("vector", lambda v: v.tensor_tensor(gap[:, 0, :], gap[:, 0, :], norm2[:, 1, :], ALU.mult),
                       s_soft)
            wait("scalar", mark)
            route["exp", u] = put("scalar", lambda a: a.activation(gap[:, 1, :], gap[:, 0, :], ACT.Exp), s_norm2)

        def places(u):
            g, t0 = u // GUNITS, u * UT
            wait("vector", route["rank", u])
            mark = put("vector", lambda v: v.tensor_tensor(
                place[:, :, :], ps_small[:, 0:UT * E].rearrange("p (i e) -> p i e", i=UT),
                region_row[:, g, :].unsqueeze(1).to_broadcast([P, UT, E]), ALU.add), s_route)
            route["place", u] = mark
            wait("vector", mark)
            for k in range(TOPK):
                mark = put("vector", lambda v, k=k: v.tensor_tensor(
                    picked[:, k, :, :], chosen[:, k, :, :], place[:, :, :], ALU.mult), s_route)
            wait("vector", mark)
            mark = put("vector", lambda v: v.tensor_reduce(
                place_f[:, :, :], picked[:, :, :, :].rearrange("p k i e -> p (k i) e"), AX_X, ALU.add), s_route)
            wait("vector", mark)
            route["rows", u] = put("vector", lambda v: v.tensor_copy(
                place_i[:, t0:t0 + UT, :], place_f[:, :, :].rearrange("p k i -> p i k")), s_route)
            wait("vector", route["exp", u])
            mark = put("vector", lambda v: v.tensor_scalar(gap[:, 2, :], gap[:, 1, :], 1.0, None, ALU.add), s_soft)
            wait("vector", mark)
            mark = put("vector", lambda v: v.reciprocal(gap[:, 0, :], gap[:, 2, :]), s_soft)
            wait("vector", mark)
            put("vector", lambda v: v.tensor_copy(weight_sb[:, t0:t0 + UT, 0], gap[:, 0, :]), s_soft)
            mark = put("vector", lambda v: v.tensor_tensor(weight_sb[:, t0:t0 + UT, 1], gap[:, 0, :], gap[:, 1, :],
                                                           ALU.mult), s_soft)
            route["free", u] = (mark, route["rank", u], (s_nmr2, s_nmr2.count), squared[t0 + UT - 1])
            for i in range(UT):
                t = t0 + i
                wait("gpsimd", route["rows", u], xn_m[t])
                scattered[t] = tuple(put("gpsimd", lambda q, k=k, t=t: q.indirect_dma_start(
                    out=sorted_x, out_offset=bass.IndirectOffsetOnAxis(ap=place_i[:, t, k:k + 1], axis=0),
                    in_=xn_sb[:, t % NSLOTS, :], in_offset=None), s_scatter[t % NSLOTS], DMA)
                    for k in range(TOPK))[-1:]

        region_row = sb("region_row", [P, GROUPS, E], F32)
        for g in range(GROUPS):
            regions = put("gpsimd", lambda q, g=g: q.iota(
                region_row[:, g, :], pattern=[[REGION * P, E]], base=g * GREG * P, channel_multiplier=0,
                allow_small_or_imprecise_dtypes=True), s_const)
        wait("vector", regions)

        def count_group(g):
            u = (g + 1) * GUNITS - 1
            wait("tensor", route["place", u])
            total = put("tensor", lambda t: t.matmul(ps_small[:, 0:E], ones_b[:, :], before_cnt[:, GTILES, :],
                                                     start=True, stop=True), s_total)
            route["total", g] = total
            wait("vector", total)
            route["counted", g] = put("vector", lambda v: v.tensor_copy(cnt_sb[:, g, :], ps_small[:, 0:E]), s_table)
            wait("vector", route["counted", g])
            mark = put("vector", lambda v: v.scalar_tensor_tensor(
                out=pad_f[:, :], in0=cnt_sb[:, g, :], scalar=float(g * GREG * P), in1=iota_p[:, :],
                op0=ALU.add, op1=ALU.add), s_table)
            wait("vector", mark)
            mark = put("vector", lambda v: v.tensor_copy(pad_i[:, g, :], pad_f[:, :]), s_table)
            wait("gpsimd", mark)
            t = (u + 1) * UT - 1
            for e in range(E):
                route["pad", g] = put("gpsimd", lambda q, e=e: q.indirect_dma_start(
                    out=sorted_x, out_offset=bass.IndirectOffsetOnAxis(ap=pad_i[:, g, e:e + 1], axis=0),
                    in_=xn_sb[:, t % NSLOTS, :], in_offset=None), s_pad, DMA)
            scattered[t] = scattered[t] + (route["pad", g],)

        for t in range(UT):
            load_tile(t)
            load_ctx(t) if t < VSLOTS else None
        for t in range(UT):
            first_norm(t)
        for t in range(UT):
            exponentials(t)
            if t + VSLOTS < UT:
                load_ctx(t + VSLOTS)
        for t in range(UT, 2 * UT):
            load_tile(t)
        for e in range(E):
            w13_in = load_w13(e)
        N = UNITS * J
        for n in range(N + 3):
            u, j = divmod(n, J)
            if n < N:
                turn(n)
            if 0 <= n - 2 < N:
                turn_back(n - 2)
            if n < N:
                turn_x(n)
                recur(n)
            if 0 <= n - 1 < N:
                add_residual(n - 1)
            if n < N:
                divide(n)
            if 0 <= n - 2 < N:
                keep_x1(n - 2)
            if j == 1 and u >= 1:
                second_norm(u - 1)
            if j == 2 and u >= 1:
                rank_tokens(u - 1)
                normed_rows(u - 1)
                places(u - 1)
                if u % GUNITS == 0:
                    count_group(u // GUNITS - 1)
            nxt = u + 1
            if nxt < UNITS:
                if j == 3:
                    if nxt >= 2:
                        for i in range(UT):
                            load_tile(nxt * UT + i)
                    for i in range(VSLOTS):
                        load_ctx(nxt * UT + i)
                if j in (3, 4):
                    for i in (0, 1):
                        first_norm(nxt * UT + (j - 3) * 2 + i)
                if 4 <= j < 4 + UT:
                    t = nxt * UT + j - 4
                    exponentials(t)
                    if j - 4 + VSLOTS < UT:
                        load_ctx(t + VSLOTS)
            if n == (UNITS - 1) * J:
                wait("gpsimd", tv[n - 1])
                for e in range(E):
                    w2_in = load_w2(e)

        end_a = [x1m[N - 1], x1t[N - 1], ym[N - 1], num[N - 1], routed_pe[N - 1], tv[N - 1],
                 *spilled.values(), xn_m[TOKENS // P - 1], ev_in[TOKENS // P - 1], *route["free", UNITS - 1]]

        def make_table(g):
            M = REGION - 1
            o = [0]

            def space(shape):
                size = 1
                for s in shape:
                    size *= s
                a = tab[:, o[0]:o[0] + size]
                o[0] += size
                return a.rearrange("p (a b) -> p a b", b=shape[-1]) if len(shape) > 1 else a

            steps, over, tiles, upto, one, kk, past, prod, row, exp_ = (
                space((M,)), space((E, M)), space((E,)), space((E,)), space((E,)), space((KT,)),
                space((KT, E)), space((KT, E)), space((KT,)), space((KT,)))
            C = GTILES * TOPK
            move, same, shift = space((E,)), space((C, E)), space((C,))
            assert o[0] <= ND * UNIT
            wait("gpsimd", *end_a, route.get(("table", g - 1)))
            put("gpsimd", lambda q: q.iota(steps, pattern=[[P, M]], base=0, channel_multiplier=0,
                                           allow_small_or_imprecise_dtypes=True), s_const)
            put("gpsimd", lambda q: q.memset(one, 1.0), s_const)
            made = put("gpsimd", lambda q: q.iota(kk, pattern=[[1, KT]], base=0, channel_multiplier=0,
                                                  allow_small_or_imprecise_dtypes=True), s_const)
            wait("vector", made)

            def step(fn):
                wait("vector", put("vector", fn, s_table))

            step(lambda v: v.tensor_tensor(over, cnt_sb[:, g, :].unsqueeze(2).to_broadcast([P, E, M]),
                                           steps.unsqueeze(1).to_broadcast([P, E, M]), ALU.is_gt))
            step(lambda v: v.tensor_reduce(tiles, over, AX_X, ALU.add))
            step(lambda v: v.tensor_tensor_scan(out=upto, data0=one, data1=tiles, initial=0.0,
                                                op0=ALU.mult, op1=ALU.add))
            step(lambda v: v.tensor_tensor(past, kk.unsqueeze(2).to_broadcast([P, KT, E]),
                                           upto.unsqueeze(1).to_broadcast([P, KT, E]), ALU.is_ge))
            step(lambda v: v.tensor_reduce(exp_, past, AX_X, ALU.add))
            step(lambda v: v.tensor_tensor(move, upto, tiles, ALU.subtract))
            step(lambda v: v.scalar_tensor_tensor(out=move, in0=move, scalar=float(P), in1=region_row[:, g, :],
                                                  op0=ALU.mult, op1=ALU.subtract))
            group_tiles = slice(g * GTILES, (g + 1) * GTILES)
            step(lambda v: v.tensor_tensor(
                same, expert_sb[:, group_tiles, :].rearrange("p t k -> p (t k)").unsqueeze(2).to_broadcast([P, C, E]),
                iota_e[:, :].unsqueeze(1).to_broadcast([P, C, E]), ALU.is_equal))
            step(lambda v: v.tensor_tensor(same, same, move.unsqueeze(1).to_broadcast([P, C, E]), ALU.mult))
            step(lambda v: v.tensor_reduce(shift, same, AX_X, ALU.add))
            wait("vector", *all_scattered)
            rows_i = place_i[:, group_tiles, :].rearrange("p t k -> p (t k)")
            step(lambda v: v.tensor_tensor(rows_i, rows_i, shift, ALU.add))
            step(lambda v: v.tensor_scalar(tiles, tiles, -1.0, float(REGION), ALU.mult, ALU.add))
            step(lambda v: v.tensor_tensor(prod, past, tiles.unsqueeze(1).to_broadcast([P, KT, E]), ALU.mult))
            step(lambda v: v.tensor_reduce(row, prod, AX_X, ALU.add))
            step(lambda v: v.tensor_tensor(row, row, kk, ALU.add))
            step(lambda v: v.tensor_scalar(table_i[:, g, 0, :], row, float(P), float(g * GREG * P),
                                           ALU.mult, ALU.add))
            route["table", g] = put("vector", lambda v: v.tensor_scalar(
                table_i[:, g, 1, :], exp_, float(E - 1), None, ALU.min), s_table)
            wait("vector", route["table", g])

        xs_in, hm, sm, gm, htm, htcm, ypm, yam, ydm, yout = {}, {}, {}, {}, {}, {}, {}, {}, {}, {}
        W13_E, W2_E = J * 2 * FF, FC * D
        all_scattered = [(s, s.count) for s in s_scatter]

        def row_of(engine, k):
            g, kk = divmod(k, KT)
            return engine.value_load(table_i[0:1, g, 0, kk:kk + 1], min_val=0,
                                     max_val=(GROUPS * GREG - 1) * P)

        def load_sorted(k):
            g = k // KT
            wait("sync", route["table", g], route["pad", g], *all_scattered, zeroed, *end_a, hm.get(k - XS))
            xs_in[k] = put("sync", lambda s: s.dma_start_transpose(
                out=xs_sb[:, k % XS, :, :], in_=sorted_x[bass.ds(row_of(s, k), P), :]), s_xs[k % XS], DMA)

        expert_of = {}

        def gate_up(k):
            g, kk = divmod(k, KT)
            wait("tensor", route["table", g], w13_in, xs_in[k], gm.get(k - 2))
            for c in range(J):
                def go(t, c=c):
                    if c == 0:
                        expert_of[k] = t.value_load(table_i[0:1, g, 1, kk:kk + 1], min_val=0, max_val=E - 1)
                    return t.matmul(bank[k % 2][:, :], xs_sb[:, k % XS, c, :],
                                    w13_sb[:, bass.ds(expert_of[k] * W13_E + c * 2 * FF, 2 * FF)],
                                    start=(c == 0), stop=(c == J - 1))
                hm[k] = put("tensor", go, s_h if c == J - 1 else None)

        def gate(k):
            wait("scalar", hm[k], gm.get(k - 2))
            sm[k] = put("scalar", lambda a: a.activation(silu_sb[:, k % 2, :], bank[k % 2][:, 0:FF], ACT.Silu), s_silu)
            wait("vector", sm[k], htm.get(k - 2))
            gm[k] = put("vector", lambda v: v.tensor_tensor(h_sb[:, k % 2, :], silu_sb[:, k % 2, :],
                                                            bank[k % 2][:, FF:2 * FF], ALU.mult), s_gate)

        def turn_h(k):
            wait("tensor", gm[k], htcm.get(k - 2))
            dst = bank[2 + k % 2][:, :].bitcast(BF16)
            for c in range(FC):
                htm[k] = put("tensor", lambda t, c=c: t.transpose(dst[:, c * P:(c + 1) * P],
                                                                  h_sb[:, k % 2, c * P:(c + 1) * P], ident_b[:, :]),
                             s_ht if c == FC - 1 else None)
            wait("vector", htm[k], ypm.get(k - 2))
            htcm[k] = put("vector", lambda v: v.tensor_copy(ht_sb[:, k % 2, :], dst[:, 0:FF]), s_htc)

        def down(k):
            wait("tensor", htcm[k], w2_in, yam.get(k - 2), ydm.get(k - 2))
            for half in range(2):
                for c in range(FC):
                    ypm[k] = put("tensor", lambda t, half=half, c=c: t.matmul(
                        bank[4 + 2 * (k % 2) + half][:, :], ht_sb[:, k % 2, c * P:(c + 1) * P],
                        w2_sb[:, bass.ds(expert_of[k] * W2_E + c * D + half * 512, 512)],
                        start=(c == 0), stop=(c == FC - 1)), s_yp if c == FC - 1 else None)
            wait("scalar", ypm[k], yout.get(k - YB))
            yam[k] = put("scalar", lambda a: a.activation(y_sb[:, k % YB, 0:512], bank[4 + 2 * (k % 2)][:, :],
                                                          ACT.Copy), s_ya)
            wait("vector", ypm[k], yout.get(k - YB))
            ydm[k] = put("vector", lambda v: v.tensor_copy(y_sb[:, k % YB, 512:D], bank[5 + 2 * (k % 2)][:, :]), s_yd)

        def store_rows(k):
            wait("sync", yam[k], ydm[k])
            yout[k] = put("sync", lambda s: s.dma_start(
                expert_y[k // KT][k % KT * P:(k % KT + 1) * P, :], y_sb[:, k % YB, :]),
                          s_yout[k % YB], DMA)

        res_in, picks, sums_m, outs = {}, {}, {}, {}

        def load_residual(t):
            wait("sync", *end_a, outs.get(t - CB))
            res_in[t] = put("sync", lambda s: s.dma_start(x_sb[:, t % CB, :], residual[t * P:(t + 1) * P, :]),
                            s_res[t % CB], DMA)

        def combine(t):
            g = t // GTILES
            wait("gpsimd", *end_a, *(yout[k] for k in range((g + 1) * KT - YB, (g + 1) * KT)), sums_m.get(t - 2))
            for k in range(TOPK):
                picks[t] = put("gpsimd", lambda q, k=k: q.indirect_dma_start(
                    out=pick_sb[:, 2 * (t % 2) + k, :], out_offset=None, in_=expert_y[g],
                    in_offset=bass.IndirectOffsetOnAxis(ap=place_i[:, t, k:k + 1], axis=0)), s_pick[t % 2], DMA)

        def add_rows(t):
            wait("vector", picks[t], res_in[t])
            for k in range(TOPK):
                sums_m[t] = put("vector", lambda v, k=k: v.scalar_tensor_tensor(
                    out=x_sb[:, t % CB, :], in0=pick_sb[:, 2 * (t % 2) + k, :], scalar=weight_sb[:, t, k:k + 1],
                    in1=x_sb[:, t % CB, :], op0=ALU.mult, op1=ALU.add), s_sum)
                wait("vector", sums_m[t])
            wait("scalar", sums_m[t])
            outs[t] = put("scalar", lambda a: a.dma_start(out_rows[t * P:(t + 1) * P, :], x_sb[:, t % CB, :]),
                          s_out[t % CB], DMA)

        second = UNITS - 1
        end_a += [*route["free", second], *(m for t in range(TOKENS // P - NSLOTS, TOKENS // P) for m in scattered[t]),
                  *(xn_m[t] for t in range(TOKENS // P - NSLOTS, TOKENS // P))]
        end_a = [m for m in end_a if m is not None]
        all_scattered = [(s, s.count) for s in s_scatter]
        for g in range(GROUPS):
            make_table(g)
        for m in range(KT * GROUPS + 4):
            if m == 0:
                for k in range(XS - 2):
                    load_sorted(k)
            if m < KT * GROUPS:
                gate_up(m)
                gate(m)
            if 0 <= m - 1 < KT * GROUPS:
                turn_h(m - 1)
            if 0 <= m - 2 < KT * GROUPS:
                down(m - 2)
                store_rows(m - 2)
            if m + XS - 2 < KT * GROUPS:
                load_sorted(m + XS - 2)
            c, odd = divmod(m - KT - 4, 2)
            if c >= 0 and not odd and c < GTILES:
                load_residual(c)
                combine(c)
            if c >= 1 and not odd and c - 1 < GTILES:
                add_rows(c - 1)
        for t in range(GTILES, TOKENS // P):
            load_residual(t)
            combine(t)
            if t > GTILES:
                add_rows(t - 1)
        add_rows(TOKENS // P - 1)
        for s in (*s_out, *s_yout, *s_spill, *s_scatter, s_pad, s_zero):
            wait("sync", (s, s.count))

        block = stack.enter_context(nc.Block())
        block.sync(lambda e: S.emit("sync", e))
        block.gpsimd(lambda e: S.emit("gpsimd", e))
        block.scalar(lambda e: S.emit("scalar", e))
        block.vector(lambda e: S.emit("vector", e))
        block.tensor(lambda e: S.emit("tensor", e))


_INS = ['x', 'ctx_2048', 'L0_xattn_w', 'L0_xattn_u', 'L0_ffn_router_w', 'L0_ffn_w1', 'L0_ffn_w2', 'L0_ffn_w3']


def kernel(**inputs):
    import numpy as _np
    import concourse.bacc as _bacc
    from concourse import mybir as _mybir
    from concourse.bass_utils import run_bass_kernel_spmd as _run

    nc = _bacc.Bacc("TRN2", target_bir_lowering=False, num_devices=1)
    arrays, args = {}, []
    for name in _INS:
        a = _np.ascontiguousarray(inputs[name])
        arrays[f"in_{name}_dram"] = a
        args.append(nc.dram_tensor(f"in_{name}_dram", a.shape, _mybir.dt.from_np(a.dtype), kind="ExternalInput").ap())
    out = nc.dram_tensor("out_0_dram", inputs['x'].shape, _mybir.dt.float32, kind="ExternalOutput").ap()
    wkv_moe(nc, *args, out)
    r = _run(nc, [arrays], core_ids=[0])
    return r.results[0]["out_0_dram"]
```

```python
from contextlib import ExitStack

import concourse.bass as bass
from concourse import mybir

ALU = mybir.AluOpType
ACT = mybir.ActivationFunctionType
AX_X = mybir.AxisListType.X
F32 = mybir.dt.float32
BF16 = mybir.dt.bfloat16
I32 = mybir.dt.int32
U32 = mybir.dt.uint32

P = 128
EPS = 1e-5
U_CAP = 50.0
DMA = 16


class Signal:

    def __init__(self, handle):
        self.handle, self.count = handle, 0


class Streams:

    def __init__(self, engines):
        self.lists = {e: [] for e in engines}
        self.passed = {}

    def put(self, engine, instruction, signal=None, by=1):
        self.lists[engine].append((instruction, signal, by))
        if signal is None:
            return None
        signal.count += by
        return signal, signal.count

    def wait(self, engine, *marks):
        for mark in marks:
            if mark is None:
                continue
            signal, value = mark
            if self.passed.get((engine, signal), 0) < value:
                self.passed[engine, signal] = value
                self.lists[engine].append((None, signal, value))

    def emit(self, name, engine):
        for instruction, signal, number in self.lists[name]:
            if instruction is None:
                engine.wait_ge(signal.handle, number)
                continue
            made = instruction(engine)
            if signal is not None:
                made.then_inc(signal.handle, number)


def wkv_moe(nc, x, ctx, decay, bonus, router, w1, w2, w3, out):
    B, T, D = x.shape
    E, _, FF = w1.shape
    TOPK = 2
    TOKENS = B * T
    UNIT = 512
    UT = UNIT // P
    UNITS = TOKENS // UNIT
    PER_ROW = T // UNIT
    J = D // P
    GROUPS = 2
    GT = TOKENS // GROUPS
    GTILES = GT // P
    GUNITS = UNITS // GROUPS
    SPARE = E - 1
    KT = GT * TOPK // P + SPARE
    REGION = GT // P + 1
    GREG = E * REGION + SPARE
    FC = FF // P
    R1 = E + 1

    x_rows = x.rearrange("b t d -> (b t) d")
    ctx_rows = ctx.rearrange("b t d -> (b t) d")
    out_rows = out.rearrange("b t d -> (b t) d")
    sorted_x = nc.dram_tensor("sorted_x", [GROUPS * GREG * P, D], BF16, kind="Internal").ap()
    expert_y = [nc.dram_tensor(f"expert_y{g}", [KT * P, D], BF16, kind="Internal").ap() for g in range(GROUPS)]
    residual = nc.dram_tensor("residual", [TOKENS, D], F32, kind="Internal").ap()

    with ExitStack() as stack:
        def sb(name, shape, dt):
            return stack.enter_context(nc.sbuf_tensor(name, shape, dt))

        def sig(name):
            return Signal(stack.enter_context(nc.semaphore(name)))

        w13_sb = sb("w13_sb", [P, E * J * 2 * FF], BF16)
        w2_sb = sb("w2_sb", [P, E * FC * D], BF16)
        XUNITS, NSLOTS = 3, 6
        XSLOTS = XUNITS * UT
        x_sb = sb("x_sb", [P, (XUNITS - 1) * UT, D], F32)
        ek_odd = sb("ek_odd", [P, 2 * UT * D], F32)
        scan_sb = sb("scan_sb", [P, 2, 2, UNIT + 1], F32)
        ND = 3
        num_sb = sb("num_sb", [P, ND, UNIT], F32)
        den_sb = sb("den_sb", [P, ND, UNIT], F32)
        x1t_sb = sb("x1t_sb", [P, 2, UNIT], F32)
        xn_sb = sb("xn_sb", [P, NSLOTS, D], BF16)
        ek_even = w2_sb[:, :].bitcast(F32)
        ek_all = [b.rearrange("p (s i d) -> p s i d", s=2, i=UT) for b in (ek_even, ek_odd[:, :])]
        LATE = UT * D * 2 // (J * 2 * FF)
        x_third = w13_sb[:, (E - LATE) * J * 2 * FF:].bitcast(F32).rearrange("p (i d) -> p i d", i=UT)
        assert UNITS % XUNITS == XUNITS - 1

        def x_unit(u):
            k = u % XUNITS
            return x_third if k == XUNITS - 1 else x_sb[:, k * UT:(k + 1) * UT, :]

        def x_tile(t):
            return x_unit(t // UT)[:, t % UT, :]


        ident = sb("ident", [P, P], F32)
        ident_b = sb("ident_b", [P, P], BF16)
        before_b = sb("before_b", [P, P], BF16)
        ones_b = sb("ones_b", [P, P], BF16)
        eps_sb = sb("eps_sb", [P, 1], F32)
        router_t = sb("router_t", [P, J, R1], F32)
        router_sum = sb("router_sum", [P, E], F32)
        chan = sb("chan", [P, 2, J], F32)
        chan_k = sb("chan_k", [P, 4, J], F32)
        state = sb("state", [P, J, 2], F32)
        stats = sb("stats", [P, 2, 12], F32)
        mv = sb("mv", [P, XSLOTS, 2], F32)
        norm1 = sb("norm1", [P, XSLOTS, 3], F32)
        sc_sb = sb("sc_sb", [P, UT, R1], F32)
        negmean = sb("negmean", [P, UT], F32)
        sumsq = sb("sumsq", [P, UT], F32)
        norm2 = sb("norm2", [P, 3, UT], F32)
        score = sb("score", [P, UT, E], F32)
        top = sb("top", [P, UT, 8], F32)
        top_i = sb("top_i", [P, UT, 8], U32)
        top_f = sb("top_f", [P, TOPK, UT], F32)
        chosen = sb("chosen", [P, TOPK, UT, E], F32)
        mask_b = sb("mask_b", [P, UT, E], BF16)
        before_cnt = sb("before_cnt", [P, GTILES + 1, E], BF16)
        gap = sb("gap", [P, 3, UT], F32)
        place = sb("place", [P, UT, E], F32)
        picked = sb("picked", [P, TOPK, UT, E], F32)
        place_f = sb("place_f", [P, TOPK, UT], F32)
        iota_e = sb("iota_e", [P, E], F32)
        iota_p = sb("iota_p", [P, E], F32)
        weight_sb = sb("weight_sb", [P, TOKENS // P, TOPK], F32)
        place_i = sb("place_i", [P, TOKENS // P, TOPK], I32)
        expert_sb = sb("expert_sb", [P, TOKENS // P, TOPK], F32)
        pad_f = sb("pad_f", [P, E], F32)
        pad_i = sb("pad_i", [P, GROUPS, E], I32)
        cnt_sb = sb("cnt_sb", [P, GROUPS, E], F32)
        table_i = sb("table_i", [P, GROUPS, 2, KT], I32)
        region_row = sb("region_row", [P, GROUPS, E], F32)
        TAB = (GTILES + 2) * E + 2 * E + 3 * KT + 2 * KT * E + 2 * E + GTILES + (E + 1) * GTILES * TOPK
        tab = sb("tab", [P, TAB], F32)

        XS, YB, PICKS = 8, 4, NSLOTS // TOPK
        ek_b = ek_odd[:, :].bitcast(BF16)
        xs_sb = ek_b[:, 0:XS * D].rearrange("p (s c t) -> p s c t", s=XS, c=J)
        y_sb = ek_b[:, XS * D:(XS + YB) * D].rearrange("p (s d) -> p s d", s=YB)
        num_b = num_sb[:, :, :].rearrange("p a b -> p (a b)").bitcast(BF16)
        silu_sb = num_b[:, 0:2 * FF].rearrange("p (s f) -> p s f", s=2)
        h_sb = num_b[:, 2 * FF:4 * FF].rearrange("p (s f) -> p s f", s=2)
        ht_sb = num_b[:, 4 * FF:6 * FF].rearrange("p (s f) -> p s f", s=2)
        pick_sb = xn_sb.rearrange("p (s k) d -> p s k d", k=TOPK)
        scan_f = scan_sb[:, :, :, :].rearrange("p a b c -> p (a b c)")
        res_slots = [ek_odd[:, (XS + YB) * D // 2 + i * D:(XS + YB) * D // 2 + (i + 1) * D] for i in range(2)]
        res_slots += [scan_f[:, 0:D], scan_f[:, D:2 * D], x1t_sb[:, :, :].rearrange("p a b -> p (a b)"),
                      den_sb[:, 0:2, :].rearrange("p a b -> p (a b)")]
        CB = len(res_slots)

        bank = [stack.enter_context(nc.psum_tensor(f"bank{i}", [P, 512], F32)) for i in range(8)]
        ps_e, ps_v, ps_x, ps_b, ps_score, ps_small = bank[0], bank[1], bank[2:4], bank[4:6], bank[6], bank[7]

        s_const, s_setup_dma, s_setup_pe, s_setup_dve, s_setup_act = map(
            sig, ("s_const", "s_setup_dma", "s_setup_pe", "s_setup_dve", "s_setup_act"))
        s_x = [sig(f"s_x_in{i}") for i in range(XSLOTS)]
        s_v = [sig(f"s_v_in{i}") for i in range(2 * UT)]
        s_spill = [sig(f"s_spill{i}") for i in range(2)]
        s_stats, s_norm1, s_nmr1, s_exp, s_ev, s_ev_dve = map(
            sig, ("s_stats", "s_norm1", "s_nmr1", "s_exp", "s_ev", "s_ev_dve"))
        s_te, s_tv, s_tx, s_router, s_back = map(sig, ("s_te", "s_tv", "s_tx", "s_router", "s_back"))
        s_scan, s_den, s_num, s_log, s_inv, s_y, s_x1t, s_x1 = map(
            sig, ("s_scan", "s_den", "s_num", "s_log", "s_inv", "s_y", "s_x1t", "s_x1"))
        s_sum_xy, s_x1t_act = sig("s_sum_xy"), sig("s_x1t_act")
        s_route, s_norm2, s_nmr2, s_soft, s_xn, s_rank = map(
            sig, ("s_route", "s_norm2", "s_nmr2", "s_soft", "s_xn", "s_rank"))
        s_scatter = [sig(f"s_scatter{i}") for i in range(NSLOTS)]
        s_pad, s_zero, s_w13 = sig("s_pad"), sig("s_zero"), sig("s_w13")
        s_w2 = sig("s_w2")
        s_table, s_total = sig("s_table"), sig("s_total")
        s_xs = [sig(f"s_xs{i}") for i in range(XS)]
        s_h, s_silu, s_gate, s_ht, s_htc, s_yp, s_ya, s_yd = map(
            sig, ("s_h", "s_silu", "s_gate", "s_ht", "s_htc", "s_yp", "s_ya", "s_yd"))
        s_yout = [sig(f"s_yout{i}") for i in range(YB)]
        s_res = [sig(f"s_res{i}") for i in range(CB)]
        s_pick = [sig(f"s_pick{i}") for i in range(PICKS)]
        s_out = [sig(f"s_out{i}") for i in range(8)]
        s_sum = sig("s_sum")

        S = Streams(("sync", "gpsimd", "scalar", "vector", "tensor"))
        put, wait = S.put, S.wait

        def diagonal(tile, compare, fill):
            made = put("gpsimd", lambda g: g.memset(tile[:, :], 1.0 - fill), s_const)
            wait("gpsimd", made)
            return put("gpsimd", lambda g: g.affine_select(
                out=tile[:, :], in_=tile[:, :], compare_op=compare, fill=fill, base=0,
                pattern=[[-1, P]], channel_multiplier=1), s_const)

        put("gpsimd", lambda g: g.memset(xn_sb[:, 0, :], 0.0), s_const)
        put("gpsimd", lambda g: g.memset(eps_sb[:, :], EPS), s_const)
        put("gpsimd", lambda g: g.memset(ones_b[:, :], 1.0), s_const)
        put("gpsimd", lambda g: g.memset(router_t[:, :, E:R1], 1.0), s_const)
        put("gpsimd", lambda g: g.memset(before_cnt[:, 0, :], 0.0), s_const)
        ones_f = x1t_sb[:, 0, 0:P]
        put("gpsimd", lambda g: g.memset(ones_f, 1.0), s_const)
        put("gpsimd", lambda g: g.iota(iota_e[:, :], pattern=[[1, E]], base=0, channel_multiplier=0,
                                       allow_small_or_imprecise_dtypes=True), s_const)
        put("gpsimd", lambda g: g.iota(iota_p[:, :], pattern=[[REGION * P, E]], base=0, channel_multiplier=1,
                                       allow_small_or_imprecise_dtypes=True), s_const)
        diagonal(ident, ALU.not_equal, 1.0)
        diagonal(ident_b, ALU.not_equal, 1.0)
        made = put("gpsimd", lambda g: g.memset(before_b[:, :], 1.0), s_const)
        wait("gpsimd", made)
        const = put("gpsimd", lambda g: g.affine_select(
            out=before_b[:, :], in_=before_b[:, :], compare_op=ALU.is_gt, fill=0.0, base=0,
            pattern=[[1, P]], channel_multiplier=-1), s_const)

        rows = den_sb[0:2 * J, 0, 0:P]
        router_rows = num_sb[0:E, 0:2, :].rearrange("p a b -> p (a b)")
        put("scalar", lambda a: a.dma_start(den_sb[0:J, 0, 0:P], decay.rearrange("(j p) -> j p", p=P)),
            s_setup_dma, DMA)
        put("scalar", lambda a: a.dma_start(den_sb[J:2 * J, 0, 0:P], bonus.rearrange("(j p) -> j p", p=P)),
            s_setup_dma, DMA)
        small_in = put("scalar", lambda a: a.dma_start(router_rows, router[:, :]), s_setup_dma, DMA)
        wait("tensor", const, small_in)
        for j in range(J):
            put("tensor", lambda t, j=j: t.transpose(ps_small[:, j * E:(j + 1) * E],
                                                     router_rows[:, j * P:(j + 1) * P], ident[0:E, 0:E]))
        turned = put("tensor", lambda t: t.transpose(ps_b[0][:, 0:2 * J], rows, ident[0:2 * J, 0:2 * J]),
                     s_setup_pe)
        wait("vector", const, turned)
        router_in = put("vector", lambda v: v.tensor_copy(
            router_t[:, :, 0:E], ps_small[:, 0:J * E].rearrange("p (j e) -> p j e", j=J)), s_setup_dve)
        put("vector", lambda v: v.tensor_copy(
            chan[:, :, :], ps_b[0][:, 0:2 * J].rearrange("p (s j) -> p s j", s=2)), s_setup_dve)
        wait("vector", (s_setup_dve, s_setup_dve.count))
        put("vector", lambda v: v.tensor_scalar(chan_k[:, 2, :], chan[:, 1, :], 0.0, -1.0, ALU.max, ALU.mult),
            s_setup_dve)
        chan_in = put("vector", lambda v: v.tensor_scalar(chan_k[:, 1, :], chan[:, 1, :], U_CAP, None, ALU.min),
                      s_setup_dve)
        put("scalar", lambda a: a.preload_act_table_set("natural_log_exp_and_others"))
        wait("scalar", chan_in)
        put("scalar", lambda a: a.activation(chan_k[:, 0, :], chan[:, 0, :], ACT.Exp), s_setup_act)
        put("scalar", lambda a: a.activation(chan_k[:, 1, :], chan_k[:, 1, :], ACT.Exp), s_setup_act)
        chan_ready = put("scalar", lambda a: a.activation(chan_k[:, 3, :], chan_k[:, 2, :], ACT.Exp), s_setup_act)
        decay_k, bonus_k, shift_k, scale_k = (chan_k[:, n, :] for n in range(4))
        wait("tensor", router_in)
        for j in range(J):
            summed = put("tensor", lambda t, j=j: t.matmul(ps_small[:, 0:E], ones_f, router_t[:, j, 0:E],
                                                           start=(j == 0), stop=(j == J - 1)),
                         s_setup_pe if j == J - 1 else None)
        wait("vector", summed)
        router_summed = put("vector", lambda v: v.tensor_copy(router_sum[:, :], ps_small[:, 0:E]), s_setup_dve)
        wait("vector", chan_ready)
        for g in range(GROUPS):
            regions = put("gpsimd", lambda q, g=g: q.iota(
                region_row[:, g, :], pattern=[[REGION * P, E]], base=g * GREG * P, channel_multiplier=0,
                allow_small_or_imprecise_dtypes=True), s_const)
        wait("vector", regions)

        wait("sync", const)
        zeroed = None
        for g in range(GROUPS):
            for t in range(SPARE):
                row = (g * GREG + E * REGION + t) * P
                zeroed = put("sync", lambda s, row=row: s.dma_start(sorted_x[row:row + P, :], xn_sb[:, 0, :]),
                             s_zero, DMA)
        w13 = w13_sb[:, :].rearrange("p (e c f) -> p e c f", e=E, c=J)
        w2v = w2_sb[:, :].rearrange("p (e c d) -> p e c d", e=E, c=FC)

        def load_w13(e, part):
            w = (w1, w3)[part]
            return put("gpsimd", lambda g: g.dma_start(
                w13[:, e, :, part * FF:(part + 1) * FF], w[e].rearrange("(c p) f -> p c f", p=P)), s_w13, DMA)

        def load_w2(e):
            return put("gpsimd", lambda g, e=e: g.dma_start(
                w2v[:, e, :, :], w2[e].rearrange("(c p) d -> p c d", p=P)), s_w2, DMA)

        x_in, v_in, stat, nrm, nmr, e_in, ev_in = {}, {}, {}, {}, {}, {}, {}
        te, tv, tx, den, num, inv, ym, x1t, x1m, routed_pe = {}, {}, {}, {}, {}, {}, {}, {}, {}, {}
        carried, scanned, added, spilled, squared, xn_m, scattered, copied_scores, route = (
            {}, {}, {}, {}, {}, {}, {}, {}, {})
        TENSOR_ADDS = (1, 2, 3, 4)
        N = UNITS * J

        def load_x(t):
            wait("sync", spilled.get(t // UT - XUNITS), xn_m.get(t - XSLOTS))
            x_in[t] = put("sync", lambda s: s.dma_start(x_tile(t), x_rows[t * P:(t + 1) * P, :]),
                          s_x[t % XSLOTS], DMA)

        def load_ctx(t):
            u, i = divmod(t, UT)
            wait("sync", tv.get((u - 2) * J + J - 1))
            v_in[t] = put("sync", lambda s: s.dma_start(ek_all[u % 2][:, 1, i, :], ctx_rows[t * P:(t + 1) * P, :]),
                          s_v[t % (2 * UT)], DMA)

        def first_norm(t):
            k = t % XSLOTS
            wait("vector", x_in[t], nmr.get(t - XSLOTS), nrm.get(t - XSLOTS))
            for h in range(2):
                mark = put("vector", lambda v, h=h: v.bn_stats(stats[:, t % 2, 6 * h:6 * h + 6],
                                                               x_tile(t)[:, h * 512:(h + 1) * 512]), s_stats)
            wait("vector", mark)
            stat[t] = put("vector", lambda v: v.bn_aggr(mv[:, k, :], stats[:, t % 2, :]), s_stats)

        def first_std(t):
            k = t % XSLOTS
            wait("scalar", stat[t], const, nmr.get(t - XSLOTS))
            mark = put("scalar", lambda a: a.activation(norm1[:, k, 0:1], mv[:, k, 1:2], ACT.Ln,
                                                        bias=eps_sb[:, 0:1]), s_norm1)
            wait("scalar", mark)
            nrm[t] = put("scalar", lambda a: a.activation(norm1[:, k, 1:2], norm1[:, k, 0:1], ACT.Exp,
                                                          scale=-0.5), s_norm1)
            wait("gpsimd", nrm[t], e_in.get(t - XSLOTS))
            nmr[t] = put("gpsimd", lambda g: g.tensor_scalar(norm1[:, k, 2:3], mv[:, k, 0:1], norm1[:, k, 1:2],
                                                             -1.0, ALU.mult, ALU.mult), s_nmr1)

        def exponential(t):
            u, i, k = t // UT, t % UT, t % XSLOTS
            wait("scalar", nmr[t], tv.get((u - 2) * J + J - 1))
            e_in[t] = put("scalar", lambda a: a.activation(ek_all[u % 2][:, 0, i, :], x_tile(t), ACT.Exp,
                                                           bias=norm1[:, k, 2:3], scale=norm1[:, k, 1:2]), s_exp)

        def weigh_ctx(t, engine="gpsimd", signal=s_ev):
            u, i = divmod(t, UT)
            wait(engine, e_in[t], v_in[t])
            buf = ek_all[u % 2]
            ev_in[t] = put(engine, lambda g: g.tensor_tensor(buf[:, 1, i, :], buf[:, 0, i, :], buf[:, 1, i, :],
                                                             ALU.mult), signal)

        def turn(n):
            u, j = divmod(n, J)
            buf = ek_all[u % 2]
            for part, (dst, marks, free, done, s) in enumerate((
                    (ps_e, e_in, den.get(n - 1), te, s_te), (ps_v, ev_in, num.get(n - 1), tv, s_tv))):
                wait("tensor", const, free)
                if j == 0:
                    wait("tensor", *(marks[u * UT + i] for i in range(UT)))
                for i in range(UT):
                    done[n] = put("tensor", lambda t, i=i, dst=dst, part=part: t.transpose(
                        dst[:, i * P:(i + 1) * P], buf[:, part, i, j * P:(j + 1) * P], ident[:, :]),
                        s if i == UT - 1 else None)

        def turn_x(n):
            u, j = divmod(n, J)
            wait("tensor", x1t.get(n - 2))
            for i in range(UT):
                tx[n] = put("tensor", lambda t, i=i: t.matmul(
                    ps_x[n % 2][:, i * P:(i + 1) * P], x_unit(u)[:, i, j * P:(j + 1) * P], ident[:, :],
                    is_transpose=True, start=(i == 0), stop=(i == UT - 1 and not on_tensor(n)),
                    skip_group_check=True), s_tx if i == UT - 1 else None)

        def scan_exp(n):
            if (n // J) % PER_ROW:
                carried[n] = put("vector", lambda v: v.tensor_copy(
                    scan_sb[:, n % 2, :, 0:1], state[:, n % J, :].unsqueeze(2)), s_scan)
            scan(n, 0, ps_e, te[n])

        def scan(n, part, src, turned_m):
            j, first = n % J, (n // J) % PER_ROW == 0
            sums = scan_sb[:, n % 2, part, :]
            wait("vector", turned_m, carried.get(n))
            if first:
                put("vector", lambda v: v.tensor_copy(sums[:, 0:1], src[:, 0:1]), s_scan)
            scanned[n, part] = put("vector", lambda v: v.tensor_tensor_scan(
                out=sums[:, 1:UNIT + 1], data0=decay_k[:, j:j + 1].to_broadcast([P, UNIT]), data1=src[:, :],
                initial=0.0 if first else sums[:, 0:1], op0=ALU.mult, op1=ALU.add), s_scan)

        def add_bonus(n, part, src, dst, signal):
            j = n % J
            wait("vector", scanned[n, part])
            return put("vector", lambda v: v.scalar_tensor_tensor(
                out=dst[:, n % ND, :], in0=src[:, :], scalar=bonus_k[:, j:j + 1],
                in1=scan_sb[:, n % 2, part, 0:UNIT], op0=ALU.mult, op1=ALU.add), signal)

        def make_den(n):
            wait("vector", ym.get(n - ND))
            den[n] = add_bonus(n, 0, ps_e, den_sb, s_den)
            scan(n, 1, ps_v, tv[n])

        def make_num(n):
            wait("vector", added.get(n - ND))
            num[n] = add_bonus(n, 1, ps_v, num_sb, s_num)
            if (n // J) % PER_ROW < PER_ROW - 1:
                put("vector", lambda v: v.tensor_copy(
                    state[:, n % J, :].unsqueeze(2), scan_sb[:, n % 2, :, UNIT:UNIT + 1]), s_scan)

        def divide(n):
            j = n % J
            wait("scalar", den[n])
            mark = put("scalar", lambda a: a.activation(den_sb[:, n % ND, :], den_sb[:, n % ND, :], ACT.Ln,
                                                        scale=scale_k[:, j:j + 1]), s_log)
            wait("scalar", mark)
            inv[n] = put("scalar", lambda a: a.activation(den_sb[:, n % ND, :], den_sb[:, n % ND, :], ACT.Exp,
                                                          bias=shift_k[:, j:j + 1], scale=-1.0), s_inv)

        def quotient(n):
            wait("gpsimd", inv[n], num[n])
            ym[n] = put("gpsimd", lambda g: g.tensor_tensor(num_sb[:, n % ND, :], num_sb[:, n % ND, :],
                                                            den_sb[:, n % ND, :], ALU.mult), s_y)

        def on_tensor(n):
            return (n + 2) % J in TENSOR_ADDS

        def add_residual(n):
            wait("vector", tx[n], ym[n], routed_pe.get(n - 2), router_summed, summed)
            x1t[n] = added[n] = put("vector", lambda v: v.tensor_tensor(
                x1t_sb[:, n % 2, :], ps_x[n % 2][:, :], num_sb[:, n % ND, :], ALU.add), s_x1t)

        def accumulate(n):
            wait("tensor", ym[n])
            added[n] = put("tensor", lambda t: t.matmul(
                ps_x[n % 2][:, :], ident[:, :], num_sb[:, n % ND, :], start=False, stop=True,
                skip_group_check=True), s_sum_xy)

        def keep_sum(n):
            wait("scalar", added[n], routed_pe.get(n - 2), summed)
            x1t[n] = put("scalar", lambda a: a.activation(x1t_sb[:, n % 2, :], ps_x[n % 2][:, :], ACT.Copy),
                         s_x1t_act)

        def turn_back(n):
            u, j = divmod(n, J)
            wait("tensor", x1t[n], x1m.get(n - 2))
            if j == 0:
                wait("tensor", copied_scores.get(u - 1))
            for i in range(UT):
                put("tensor", lambda t, i=i: t.matmul(
                    ps_score[:, i * R1:(i + 1) * R1], x1t_sb[:, n % 2, i * P:(i + 1) * P],
                    router_t[:, j, :], start=(j == 0 and i == 0), stop=(j == J - 1), skip_group_check=True))
            for i in range(UT):
                routed_pe[n] = put("tensor", lambda t, i=i: t.transpose(
                    ps_b[n % 2][:, i * P:(i + 1) * P], x1t_sb[:, n % 2, i * P:(i + 1) * P], ident[:, :]),
                    s_back if i == UT - 1 else None)

        def keep_x1(n):
            u, j = divmod(n, J)
            wait("scalar", routed_pe[n])
            x1m[n] = put("scalar", lambda a: a.activation(
                x_unit(u)[:, :, j * P:(j + 1) * P],
                ps_b[n % 2][:, :].rearrange("p (i c) -> p i c", i=UT), ACT.Copy), s_x1)

        def spill(u):
            wait("sync", x1m[u * J + J - 1])
            spilled[u] = put("sync", lambda s: s.dma_start(
                residual[u * UNIT:(u + 1) * UNIT, :].rearrange("(i p) d -> p i d", p=P), x_unit(u)),
                s_spill[u % 2], DMA)

        def second_mean(u):
            wait("vector", routed_pe[u * J + J - 1], xn_m.get((u - 1) * UT + UT - 1))
            copied_scores[u] = put("vector", lambda v: v.tensor_copy(
                sc_sb[:, :, :], ps_score[:, 0:UT * R1].rearrange("p (i e) -> p i e", i=UT)), s_route)
            wait("vector", copied_scores[u])
            route["mean", u] = put("vector", lambda v: v.tensor_scalar(negmean[:, :], sc_sb[:, :, E], -1.0 / D,
                                                                       None, ALU.mult), s_route)

        def square(t):
            u, i = divmod(t, UT)
            wait("scalar", x1m[u * J + J - 1], route["mean", u], *scattered.get(t - NSLOTS, ()))
            if t < NSLOTS:
                wait("scalar", zeroed)
            squared[t] = put("scalar", lambda a: a.activation(
                xn_sb[:, t % NSLOTS, :], x_tile(t), ACT.Square, bias=negmean[:, i:i + 1],
                accum_out=sumsq[:, i:i + 1]), s_norm2)

        def second_std(u):
            wait("scalar", squared[u * UT + UT - 1], route.get(("soft", u - 1)))
            mark = put("scalar", lambda a: a.activation(norm2[:, 0, :], sumsq[:, :], ACT.Ln, scale=1.0 / D,
                                                        bias=eps_sb[:, 0:1]), s_norm2)
            wait("scalar", mark)
            route["std", u] = put("scalar", lambda a: a.activation(norm2[:, 1, :], norm2[:, 0, :], ACT.Exp,
                                                                   scale=-0.5), s_norm2)
            wait("vector", route["std", u])
            route["nmr", u] = put("vector", lambda v: v.tensor_tensor(norm2[:, 2, :], negmean[:, :], norm2[:, 1, :],
                                                                      ALU.mult), s_nmr2)

        def best_two(u):
            wait("vector", route["mean", u])
            for i in range(UT):
                mark = put("vector", lambda v, i=i: v.scalar_tensor_tensor(
                    out=score[:, i, :], in0=router_sum[:, :], scalar=negmean[:, i:i + 1],
                    in1=sc_sb[:, i, 0:E], op0=ALU.mult, op1=ALU.add), s_route)
            wait("vector", mark)
            for i in range(UT):
                mark = put("vector", lambda v, i=i: v.max(top[:, i, :], score[:, i, :]), s_route)
            wait("vector", mark)
            for i in range(UT):
                mark = put("vector", lambda v, i=i: v.max_index(top_i[:, i, :], top[:, i, :], score[:, i, :]),
                           s_route)
            route["best", u] = mark

        def choices(u):
            wait("vector", route["best", u])
            mark = put("vector", lambda v: v.tensor_copy(
                top_f[:, :, :], top_i[:, :, 0:TOPK].rearrange("p i k -> p k i")), s_route)
            wait("vector", mark)
            put("vector", lambda v: v.tensor_copy(
                expert_sb[:, u * UT:(u + 1) * UT, :], top_f[:, :, :].rearrange("p k i -> p i k")), s_route)
            for k in range(TOPK):
                mark = put("vector", lambda v, k=k: v.tensor_tensor(
                    chosen[:, k, :, :], iota_e[:, :].unsqueeze(1).to_broadcast([P, UT, E]),
                    top_f[:, k, :].unsqueeze(2).to_broadcast([P, UT, E]), ALU.is_equal), s_route)
            wait("vector", mark, route.get(("rank", u - 1)))
            mark = put("vector", lambda v: v.tensor_tensor(mask_b[:, :, :], chosen[:, 0, :, :], chosen[:, 1, :, :],
                                                           ALU.add), s_route)
            for i in range(UT):
                g = (u % GUNITS) * UT + i
                wait("vector", mark)
                if g == 0:
                    wait("vector", route.get(("total", u // GUNITS - 1)))
                mark = put("vector", lambda v, i=i, g=g: v.tensor_tensor(
                    before_cnt[:, g + 1, :], before_cnt[:, g, :], mask_b[:, i, :], ALU.add), s_route)
            route["mask", u] = mark

        def rank_tokens(u):
            wait("tensor", route["mask", u], route.get(("place", u - 1)), router_summed,
                 route.get(("counted", u // GUNITS - 1)))
            for i in range(UT):
                g = (u % GUNITS) * UT + i
                dst = ps_small[:, i * E:(i + 1) * E]
                put("tensor", lambda t, i=i, dst=dst: t.matmul(dst, before_b[:, :], mask_b[:, i, :],
                                                               start=True, stop=False, skip_group_check=True))
                route["rank", u] = put("tensor", lambda t, g=g, dst=dst: t.matmul(
                    dst, ones_b[:, :], before_cnt[:, g, :], start=False, stop=True, skip_group_check=True),
                    s_rank)

        def normed_row(t):
            u, i = divmod(t, UT)
            wait("scalar", route["nmr", u], squared[t])
            xn_m[t] = put("scalar", lambda a: a.activation(
                xn_sb[:, t % NSLOTS, :], x_tile(t), ACT.Identity, bias=norm2[:, 2, i:i + 1],
                scale=norm2[:, 1, i:i + 1]), s_xn)

        def score_gap(u):
            wait("vector", route["std", u])
            mark = put("vector", lambda v: v.tensor_tensor(gap[:, 0, :], top[:, :, 1], top[:, :, 0], ALU.subtract),
                       s_soft)
            wait("vector", mark)
            mark = put("vector", lambda v: v.tensor_tensor(gap[:, 0, :], gap[:, 0, :], norm2[:, 1, :], ALU.mult),
                       s_soft)
            wait("scalar", mark)
            route["exp", u] = put("scalar", lambda a: a.activation(gap[:, 1, :], gap[:, 0, :], ACT.Exp), s_norm2)

        def places(u):
            g, t0 = u // GUNITS, u * UT
            wait("vector", route["rank", u])
            mark = put("vector", lambda v: v.tensor_tensor(
                place[:, :, :], ps_small[:, 0:UT * E].rearrange("p (i e) -> p i e", i=UT),
                region_row[:, g, :].unsqueeze(1).to_broadcast([P, UT, E]), ALU.add), s_route)
            route["place", u] = mark
            wait("vector", mark)
            for k in range(TOPK):
                mark = put("vector", lambda v, k=k: v.tensor_tensor(
                    picked[:, k, :, :], chosen[:, k, :, :], place[:, :, :], ALU.mult), s_route)
            wait("vector", mark)
            mark = put("vector", lambda v: v.tensor_reduce(
                place_f[:, :, :], picked[:, :, :, :].rearrange("p k i e -> p (k i) e"), AX_X, ALU.add), s_route)
            wait("vector", mark)
            route["rows", u] = put("vector", lambda v: v.tensor_copy(
                place_i[:, t0:t0 + UT, :], place_f[:, :, :].rearrange("p k i -> p i k")), s_route)

        def weights(u):
            t0 = u * UT
            wait("vector", route["exp", u])
            mark = put("vector", lambda v: v.tensor_scalar(gap[:, 2, :], gap[:, 1, :], 1.0, None, ALU.add), s_soft)
            wait("vector", mark)
            mark = put("vector", lambda v: v.reciprocal(gap[:, 0, :], gap[:, 2, :]), s_soft)
            wait("vector", mark)
            put("vector", lambda v: v.tensor_copy(weight_sb[:, t0:t0 + UT, 0], gap[:, 0, :]), s_soft)
            route["soft", u] = put("vector", lambda v: v.tensor_tensor(
                weight_sb[:, t0:t0 + UT, 1], gap[:, 0, :], gap[:, 1, :], ALU.mult), s_soft)

        def scatter(t, k):
            wait("gpsimd", route["rows", t // UT], xn_m[t])
            scattered[t] = (put("gpsimd", lambda q: q.indirect_dma_start(
                out=sorted_x, out_offset=bass.IndirectOffsetOnAxis(ap=place_i[:, t, k:k + 1], axis=0),
                in_=xn_sb[:, t % NSLOTS, :], in_offset=None), s_scatter[t % NSLOTS], DMA),)

        def count_group(g):
            u = (g + 1) * GUNITS - 1
            wait("tensor", route["place", u], route["mask", u])
            route["total", g] = put("tensor", lambda t: t.matmul(
                ps_small[:, 0:E], ones_b[:, :], before_cnt[:, GTILES, :], start=True, stop=True), s_total)
            wait("vector", route["total", g])
            route["counted", g] = put("vector", lambda v: v.tensor_copy(cnt_sb[:, g, :], ps_small[:, 0:E]), s_table)
            wait("vector", route["counted", g])
            mark = put("vector", lambda v: v.scalar_tensor_tensor(
                out=pad_f[:, :], in0=cnt_sb[:, g, :], scalar=float(g * GREG * P), in1=iota_p[:, :],
                op0=ALU.add, op1=ALU.add), s_table)
            wait("vector", mark)
            route["pad rows", g] = put("vector", lambda v: v.tensor_copy(pad_i[:, g, :], pad_f[:, :]), s_table)

        def pad_expert(g, e):
            t = (g + 1) * GTILES - 1
            wait("gpsimd", route["pad rows", g], xn_m[t])
            route["pad", g] = put("gpsimd", lambda q: q.indirect_dma_start(
                out=sorted_x, out_offset=bass.IndirectOffsetOnAxis(ap=pad_i[:, g, e:e + 1], axis=0),
                in_=xn_sb[:, t % NSLOTS, :], in_offset=None), s_pad, DMA)
            if e == E - 1:
                scattered[t] = scattered[t] + (route["pad", g],)

        def group_scattered(g):
            last = (g + 1) * GTILES
            return [scattered[t][0] for t in range(last - NSLOTS, last)]

        def table_steps(g):
            M = REGION - 1
            o = [0]

            def space(shape):
                size = 1
                for s in shape:
                    size *= s
                a = tab[:, o[0]:o[0] + size]
                o[0] += size
                return a.rearrange("p (a b) -> p a b", b=shape[-1]) if len(shape) > 1 else a

            steps, over, tiles, upto, one, kk, past, prod, row, exp_ = (
                space((M,)), space((E, M)), space((E,)), space((E,)), space((E,)), space((KT,)),
                space((KT, E)), space((KT, E)), space((KT,)), space((KT,)))
            C = GTILES * TOPK
            move, same, shift = space((E,)), space((C, E)), space((C,))
            assert o[0] <= TAB
            made = []

            def constants():
                wait("gpsimd", route.get(("table", g - 1)), route["counted", g])
                put("gpsimd", lambda q: q.iota(steps, pattern=[[P, M]], base=0, channel_multiplier=0,
                                               allow_small_or_imprecise_dtypes=True), s_const)
                put("gpsimd", lambda q: q.memset(one, 1.0), s_const)
                made.append(put("gpsimd", lambda q: q.iota(kk, pattern=[[1, KT]], base=0, channel_multiplier=0,
                                                           allow_small_or_imprecise_dtypes=True), s_const))

            rows_i = place_i[:, g * GTILES:(g + 1) * GTILES, :].rearrange("p t k -> p (t k)")
            group_experts = expert_sb[:, g * GTILES:(g + 1) * GTILES, :].rearrange("p t k -> p (t k)")
            arithmetic = [
                lambda v: v.tensor_tensor(over, cnt_sb[:, g, :].unsqueeze(2).to_broadcast([P, E, M]),
                                          steps.unsqueeze(1).to_broadcast([P, E, M]), ALU.is_gt),
                lambda v: v.tensor_reduce(tiles, over, AX_X, ALU.add),
                lambda v: v.tensor_tensor_scan(out=upto, data0=one, data1=tiles, initial=0.0,
                                               op0=ALU.mult, op1=ALU.add),
                lambda v: v.tensor_tensor(past, kk.unsqueeze(2).to_broadcast([P, KT, E]),
                                          upto.unsqueeze(1).to_broadcast([P, KT, E]), ALU.is_ge),
                lambda v: v.tensor_reduce(exp_, past, AX_X, ALU.add),
                lambda v: v.tensor_tensor(move, upto, tiles, ALU.subtract),
                lambda v: v.scalar_tensor_tensor(out=move, in0=move, scalar=float(P), in1=region_row[:, g, :],
                                                 op0=ALU.mult, op1=ALU.subtract),
                lambda v: v.tensor_tensor(same, group_experts.unsqueeze(2).to_broadcast([P, C, E]),
                                          iota_e[:, :].unsqueeze(1).to_broadcast([P, C, E]), ALU.is_equal),
                lambda v: v.tensor_tensor(same, same, move.unsqueeze(1).to_broadcast([P, C, E]), ALU.mult),
                lambda v: v.tensor_reduce(shift, same, AX_X, ALU.add),
                lambda v: v.tensor_scalar(tiles, tiles, -1.0, float(REGION), ALU.mult, ALU.add),
                lambda v: v.tensor_tensor(prod, past, tiles.unsqueeze(1).to_broadcast([P, KT, E]), ALU.mult),
                lambda v: v.tensor_reduce(row, prod, AX_X, ALU.add),
                lambda v: v.tensor_tensor(row, row, kk, ALU.add),
                lambda v: v.tensor_scalar(table_i[:, g, 0, :], row, float(P), float(g * GREG * P),
                                          ALU.mult, ALU.add),
                lambda v: v.tensor_scalar(table_i[:, g, 1, :], exp_, float(E - 1), None, ALU.min)]

            def step(fn):
                wait("vector", made[0])
                route["table", g] = put("vector", fn, s_table)
                wait("vector", route["table", g])

            def shift_rows():
                wait("vector", *group_scattered(g))
                route["shifted", g] = put("vector", lambda v: v.tensor_tensor(rows_i, rows_i, shift, ALU.add),
                                          s_table)
            return [constants] + [lambda fn=fn: step(fn) for fn in arithmetic] + [shift_rows]

        dispatched = {}
        SCATTERS = {8: 3, 9: 3, 10: 2}
        PADS = {11: 1, 14: 1, 15: 3, 18: 2, 19: 1}

        def finish(u, j):
            t0 = u * UT
            if j == 4:
                if u < UNITS - 2:
                    spill(u)
                best_two(u)
                square(t0)
            if j == 5:
                choices(u)
                square(t0 + 1)
                square(t0 + 2)
            if j == 6:
                rank_tokens(u)
                square(t0 + 3)
                second_std(u)
                score_gap(u)
                places(u)
            if j == 7:
                normed_row(t0)
                normed_row(t0 + 1)
                if u % GUNITS == GUNITS - 1:
                    count_group(u // GUNITS)
                weights(u)
            if j == 8:
                normed_row(t0 + 2)
                normed_row(t0 + 3)
            for _ in range(SCATTERS.get(j, 0)):
                i, k = divmod(dispatched.setdefault(("scatters", u), 0), TOPK)
                scatter(t0 + i, k)
                dispatched["scatters", u] += 1
            if u % GUNITS == GUNITS - 1:
                for _ in range(PADS.get(j, 0)):
                    pad_expert(u // GUNITS, dispatched.setdefault(("pads", u), 0))
                    dispatched["pads", u] += 1

        def prepare(u, j):
            t0 = u * UT
            if 1 <= j < 1 + UT:
                first_norm(t0 + j - 1)
                first_std(t0 + j - 1)
            if 2 <= j < 2 + UT:
                exponential(t0 + j - 2)
            if 3 <= j < 3 + UT:
                weigh_ctx(t0 + j - 3)

        for t in range(UT):
            load_x(t)
        for t in range(UT):
            load_ctx(t)
        for t in range(UT, 2 * UT):
            load_x(t)
        for t in range(UT, 2 * UT):
            load_ctx(t)
        for t in range(2 * UT, 3 * UT):
            load_x(t)
        for t in range(UT):
            first_norm(t)
            first_std(t)
            exponential(t)
        for t in range(UT):
            weigh_ctx(t) if t % 2 == 0 else weigh_ctx(t, "vector", s_ev_dve)
        late = [(e, part) for e in range(E - LATE) for part in range(2)]
        table = []
        FLUSH = 4
        for n in range(N + FLUSH):
            u, j = divmod(n, J)
            if n < N:
                turn(n)
                scan_exp(n)
            if u >= 1 and j == 3:
                second_mean(u - 1)
            if 0 <= n - 1 < N:
                quotient(n - 1)
            if 0 <= n - 2 < N:
                accumulate(n - 2) if on_tensor(n - 2) else add_residual(n - 2)
            if 0 <= n - 1 < N:
                turn_x(n - 1)
            if 0 <= n - 3 < N:
                turn_back(n - 3)
            if n < N:
                make_den(n)
            if 0 <= n - 4 < N:
                keep_x1(n - 4)
            for age in range(1, 4):
                if u >= age:
                    finish(u - age, j + (age - 1) * J)
            if u + 1 < UNITS:
                prepare(u + 1, j)
            if 0 <= n - 2 < N and on_tensor(n - 2):
                keep_sum(n - 2)
            if n < N:
                make_num(n)
                divide(n)
            if j == 7 and 3 <= u + 2 < UNITS:
                load_x((u + 2) * UT)
                load_x((u + 2) * UT + 1)
            if j == 0 and 3 <= u + 1 < UNITS:
                load_x((u + 1) * UT + 2)
                load_x((u + 1) * UT + 3)
            if j == 1 and 2 <= u + 1 < UNITS:
                for i in range(UT):
                    load_ctx((u + 1) * UT + i)
            if late and n >= 2:
                load_w13(*late.pop(0))
            if n == (GUNITS + 2) * J:
                table = table_steps(0)
            if n == (UNITS - 1) * J + 1:
                wait("gpsimd", xn_m[(UNITS - 2) * UT - 1], spilled[UNITS - 3], tv[n - 2])
            if u == UNITS - 1 and j in (1, 2):
                w13_in = load_w13(E - LATE + j - 1, 0), load_w13(E - LATE + j - 1, 1)
            if u == UNITS - 1 and 3 <= j < 3 + E // 2:
                w2_in = load_w2(2 * (j - 3)), load_w2(2 * (j - 3) + 1)
            for _ in range(3):
                if table:
                    table.pop(0)()

        xs_in, hm, sm, gm, htm, htcm, ypm, yam, ydm, yout = {}, {}, {}, {}, {}, {}, {}, {}, {}, {}
        W13_E, W2_E = J * 2 * FF, FC * D
        KTS = KT * GROUPS
        left_ek, left_e_v, left_x, left_back = tv[N - 1], num[N - 1], x1t[N - 1], x1m[N - 1]
        left_num = added[N - 1], added[N - 2], added[N - 3]

        def row_of(engine, k):
            g, kk = divmod(k, KT)
            return engine.value_load(table_i[0:1, g, 0, kk:kk + 1], min_val=0,
                                     max_val=(GROUPS * GREG - 1) * P)

        def load_sorted(k):
            g = k // KT
            wait("sync", route["table", g], route["pad", g], *group_scattered(g), zeroed, left_ek, hm.get(k - XS))
            xs_in[k] = put("sync", lambda s: s.dma_start_transpose(
                out=xs_sb[:, k % XS, :, :], in_=sorted_x[bass.ds(row_of(s, k), P), :]), s_xs[k % XS], DMA)

        expert_of = {}

        def gate_up(k):
            g, kk = divmod(k, KT)
            wait("tensor", route["table", g], *w13_in, xs_in[k], left_e_v, gm.get(k - 2))
            for c in range(J):
                def go(t, c=c):
                    if c == 0:
                        expert_of[k] = t.value_load(table_i[0:1, g, 1, kk:kk + 1], min_val=0, max_val=E - 1)
                    return t.matmul(bank[k % 2][:, :], xs_sb[:, k % XS, c, :],
                                    w13_sb[:, bass.ds(expert_of[k] * W13_E + c * 2 * FF, 2 * FF)],
                                    start=(c == 0), stop=(c == J - 1))
                hm[k] = put("tensor", go, s_h if c == J - 1 else None)

        def gate(k):
            wait("scalar", hm[k], gm.get(k - 2), *left_num)
            sm[k] = put("scalar", lambda a: a.activation(silu_sb[:, k % 2, :], bank[k % 2][:, 0:FF], ACT.Silu), s_silu)
            wait("vector", sm[k], htm.get(k - 2))
            gm[k] = put("vector", lambda v: v.tensor_tensor(h_sb[:, k % 2, :], silu_sb[:, k % 2, :],
                                                            bank[k % 2][:, FF:2 * FF], ALU.mult), s_gate)

        def turn_h(k):
            wait("tensor", gm[k], htcm.get(k - 2), left_x, x1t[N - 2])
            dst = bank[2 + k % 2][:, :].bitcast(BF16)
            for c in range(FC):
                htm[k] = put("tensor", lambda t, c=c: t.transpose(dst[:, c * P:(c + 1) * P],
                                                                  h_sb[:, k % 2, c * P:(c + 1) * P], ident_b[:, :]),
                             s_ht if c == FC - 1 else None)
            wait("vector", htm[k], ypm.get(k - 2))
            htcm[k] = put("vector", lambda v: v.tensor_copy(ht_sb[:, k % 2, :], dst[:, 0:FF]), s_htc)

        def down(k):
            wait("tensor", htcm[k], *w2_in, left_back, x1m[N - 2], yam.get(k - 2), ydm.get(k - 2))
            if k == 1:
                wait("tensor", route["counted", GROUPS - 1], copied_scores[UNITS - 1])
            for half in range(2):
                for c in range(FC):
                    ypm[k] = put("tensor", lambda t, half=half, c=c: t.matmul(
                        bank[4 + 2 * (k % 2) + half][:, :], ht_sb[:, k % 2, c * P:(c + 1) * P],
                        w2_sb[:, bass.ds(expert_of[k] * W2_E + c * D + half * 512, 512)],
                        start=(c == 0), stop=(c == FC - 1)), s_yp if c == FC - 1 else None)
            wait("scalar", ypm[k], yout.get(k - YB))
            yam[k] = put("scalar", lambda a: a.activation(y_sb[:, k % YB, 0:512], bank[4 + 2 * (k % 2)][:, :],
                                                          ACT.Copy), s_ya)
            wait("vector", ypm[k], yout.get(k - YB))
            ydm[k] = put("vector", lambda v: v.tensor_copy(y_sb[:, k % YB, 512:D], bank[5 + 2 * (k % 2)][:, :]), s_yd)

        def store_rows(k):
            wait("sync", yam[k], ydm[k])
            yout[k] = put("sync", lambda s: s.dma_start(
                expert_y[k // KT][k % KT * P:(k % KT + 1) * P, :], y_sb[:, k % YB, :]),
                          s_yout[k % YB], DMA)

        res_in, picks, sums_m, outs = {}, {}, {}, {}
        KEPT = (UNITS - 2) * UT

        def res_slot(t):
            return res_slots[t % CB] if t < KEPT else x_tile(t)

        def load_residual(t):
            if t < KEPT:
                wait("sync", num[N - 1], ym[N - 1], routed_pe[N - 1], *spilled.values(), outs.get(t - CB))
                res_in[t] = put("sync", lambda s: s.dma_start(res_slot(t), residual[t * P:(t + 1) * P, :]),
                                s_res[t % CB], DMA)

        def pick(t):
            g = t // GTILES
            wait("gpsimd", *(yout[k] for k in range((g + 1) * KT - YB, (g + 1) * KT)), sums_m.get(t - PICKS),
                 route["shifted", g])
            if t < PICKS:
                wait("gpsimd", *group_scattered(GROUPS - 1), route["pad", GROUPS - 1])
            for k in range(TOPK):
                picks[t] = put("gpsimd", lambda q, k=k: q.indirect_dma_start(
                    out=pick_sb[:, t % PICKS, k, :], out_offset=None, in_=expert_y[g],
                    in_offset=bass.IndirectOffsetOnAxis(ap=place_i[:, t, k:k + 1], axis=0)), s_pick[t % PICKS], DMA)

        def add_rows(t):
            wait("vector", picks[t], res_in.get(t))
            if t == KEPT:
                wait("vector", *(xn_m[t] for t in range(KEPT, TOKENS // P)))
            for k in range(TOPK):
                sums_m[t] = put("vector", lambda v, k=k: v.scalar_tensor_tensor(
                    out=res_slot(t), in0=pick_sb[:, t % PICKS, k, :], scalar=weight_sb[:, t, k:k + 1],
                    in1=res_slot(t), op0=ALU.mult, op1=ALU.add), s_sum)
                wait("vector", sums_m[t])
            wait("scalar", sums_m[t])
            slot = t % CB if t < KEPT else CB + t % 2
            outs[t] = put("scalar", lambda a: a.dma_start(out_rows[t * P:(t + 1) * P, :], res_slot(t)),
                          s_out[slot], DMA)

        AHEAD = XS - 2
        last = UNITS - 1
        for k in range(AHEAD):
            load_sorted(k)
        first_table = KT // 2
        for m in range(KTS + 3):
            if m < KTS:
                gate_up(m)
            finish(last, 2 * m + FLUSH)
            finish(last, 2 * m + 1 + FLUSH)
            if m == first_table:
                table = table_steps(GROUPS - 1)
            if table:
                table.pop(0)()
                table.pop(0)() if table else None
            if m < KTS:
                gate(m)
            if 0 <= m - 1 < KTS:
                turn_h(m - 1)
            if 0 <= m - 2 < KTS:
                down(m - 2)
                store_rows(m - 2)
            if m + AHEAD < KTS:
                load_sorted(m + AHEAD)
            if m == KT - 2:
                for t in range(CB):
                    load_residual(t)
            c, odd = divmod(m - KT - 3, 2)
            if c >= 0 and not odd and c < GTILES:
                pick(c)
            if c >= 1 and not odd and c - 1 < GTILES:
                add_rows(c - 1)
                load_residual(c - 1 + CB)
        for t in range(GTILES, TOKENS // P):
            pick(t)
            if t > GTILES:
                add_rows(t - 1)
                load_residual(t - 1 + CB)
        add_rows(TOKENS // P - 1)
        for s in (*s_out, *s_yout, *s_spill, *s_scatter, s_pad, s_zero):
            wait("sync", (s, s.count))

        block = stack.enter_context(nc.Block())
        block.sync(lambda e: S.emit("sync", e))
        block.gpsimd(lambda e: S.emit("gpsimd", e))
        block.scalar(lambda e: S.emit("scalar", e))
        block.vector(lambda e: S.emit("vector", e))
        block.tensor(lambda e: S.emit("tensor", e))


_INS = ['x', 'ctx_2048', 'L0_xattn_w', 'L0_xattn_u', 'L0_ffn_router_w', 'L0_ffn_w1', 'L0_ffn_w2', 'L0_ffn_w3']


def kernel(**inputs):
    import numpy as _np
    import concourse.bacc as _bacc
    from concourse import mybir as _mybir
    from concourse.bass_utils import run_bass_kernel_spmd as _run

    nc = _bacc.Bacc("TRN2", target_bir_lowering=False, num_devices=1)
    arrays, args = {}, []
    for name in _INS:
        a = _np.ascontiguousarray(inputs[name])
        arrays[f"in_{name}_dram"] = a
        args.append(nc.dram_tensor(f"in_{name}_dram", a.shape, _mybir.dt.from_np(a.dtype), kind="ExternalInput").ap())
    out = nc.dram_tensor("out_0_dram", inputs['x'].shape, _mybir.dt.float32, kind="ExternalOutput").ap()
    wkv_moe(nc, *args, out)
    r = _run(nc, [arrays], core_ids=[0])
    return r.results[0]["out_0_dram"]
```

```python
from contextlib import ExitStack

import concourse.bass as bass
from concourse import mybir

ALU = mybir.AluOpType
ACT = mybir.ActivationFunctionType
AX_X = mybir.AxisListType.X
F32 = mybir.dt.float32
BF16 = mybir.dt.bfloat16
I32 = mybir.dt.int32
U32 = mybir.dt.uint32

P = 128
EPS = 1e-5
U_CAP = 50.0
DMA = 16


class Signal:

    def __init__(self, handle):
        self.handle, self.count = handle, 0


class Streams:

    def __init__(self, engines):
        self.lists = {e: [] for e in engines}
        self.passed = {}

    def put(self, engine, instruction, signal=None, by=1):
        self.lists[engine].append((instruction, signal, by))
        if signal is None:
            return None
        signal.count += by
        return signal, signal.count

    def wait(self, engine, *marks):
        for mark in marks:
            if mark is None:
                continue
            signal, value = mark
            if self.passed.get((engine, signal), 0) < value:
                self.passed[engine, signal] = value
                self.lists[engine].append((None, signal, value))

    def emit(self, name, engine):
        for instruction, signal, number in self.lists[name]:
            if instruction is None:
                engine.wait_ge(signal.handle, number)
                continue
            made = instruction(engine)
            if signal is not None:
                made.then_inc(signal.handle, number)


def wkv_moe(nc, x, ctx, decay, bonus, router, w1, w2, w3, out):
    B, T, D = x.shape
    E, _, FF = w1.shape
    TOPK = 2
    TOKENS = B * T
    UNIT = 512
    UT = UNIT // P
    UNITS = TOKENS // UNIT
    PER_ROW = T // UNIT
    J = D // P
    GROUPS = 2
    GT = TOKENS // GROUPS
    GTILES = GT // P
    GUNITS = UNITS // GROUPS
    KT = GT * TOPK // P + E - 1
    REGION = GT // P + 1
    GREG = E * REGION
    FC = FF // P
    R1 = E + 1

    x_rows = x.rearrange("b t d -> (b t) d")
    ctx_rows = ctx.rearrange("b t d -> (b t) d")
    out_rows = out.rearrange("b t d -> (b t) d")
    sorted_x = nc.dram_tensor("sorted_x", [GROUPS * GREG * P, D], BF16, kind="Internal").ap()
    expert_y = [nc.dram_tensor(f"expert_y{g}", [KT * P, D], BF16, kind="Internal").ap() for g in range(GROUPS)]
    residual = nc.dram_tensor("residual", [TOKENS, D], F32, kind="Internal").ap()

    with ExitStack() as stack:
        def sb(name, shape, dt):
            return stack.enter_context(nc.sbuf_tensor(name, shape, dt))

        def sig(name):
            return Signal(stack.enter_context(nc.semaphore(name)))

        w13_sb = sb("w13_sb", [P, E * J * 2 * FF], BF16)
        w2_sb = sb("w2_sb", [P, E * FC * D], BF16)
        XUNITS, NSLOTS = 3, 6
        XSLOTS = XUNITS * UT
        x_sb = sb("x_sb", [P, (XUNITS - 1) * UT, D], F32)
        ek_odd = sb("ek_odd", [P, 2 * UT * D], F32)
        scan_sb = sb("scan_sb", [P, 2, 2, UNIT + 1], F32)
        ND = 3
        num_sb = sb("num_sb", [P, ND, UNIT], F32)
        den_sb = sb("den_sb", [P, ND, UNIT], F32)
        x1t_sb = sb("x1t_sb", [P, 2, UNIT], F32)
        xn_sb = sb("xn_sb", [P, NSLOTS, D], BF16)
        ek_even = w2_sb[:, :].bitcast(F32)
        ek_all = [b.rearrange("p (s i d) -> p s i d", s=2, i=UT) for b in (ek_even, ek_odd[:, :])]
        LATE = UT * D * 2 // (J * 2 * FF)
        x_third = w13_sb[:, (E - LATE) * J * 2 * FF:].bitcast(F32).rearrange("p (i d) -> p i d", i=UT)
        assert UNITS % XUNITS == XUNITS - 1

        def x_unit(u):
            k = u % XUNITS
            return x_third if k == XUNITS - 1 else x_sb[:, k * UT:(k + 1) * UT, :]

        def x_tile(t):
            return x_unit(t // UT)[:, t % UT, :]

        ident = sb("ident", [P, P], F32)
        zero_b = sb("zero_b", [P, D], BF16)
        ident_b = sb("ident_b", [P, P], BF16)
        before_b = sb("before_b", [P, P], BF16)
        ones_b = sb("ones_b", [P, P], BF16)
        eps_sb = sb("eps_sb", [P, 1], F32)
        router_t = sb("router_t", [P, J, R1], F32)
        router_sum = sb("router_sum", [P, E], F32)
        chan = sb("chan", [P, 2, J], F32)
        chan_k = sb("chan_k", [P, 4, J], F32)
        state = sb("state", [P, J, 2], F32)
        stats = sb("stats", [P, 2, 12], F32)
        mv = sb("mv", [P, XSLOTS, 2], F32)
        norm1 = sb("norm1", [P, XSLOTS, 3], F32)
        sc_sb = sb("sc_sb", [P, UT, R1], F32)
        negmean = sb("negmean", [P, UT], F32)
        sumsq = sb("sumsq", [P, UT], F32)
        norm2 = sb("norm2", [P, 3, UT], F32)
        score = sb("score", [P, UT, E], F32)
        top = sb("top", [P, UT, 8], F32)
        top_i = sb("top_i", [P, UT, 8], U32)
        top_f = sb("top_f", [P, TOPK, UT], F32)
        chosen = sb("chosen", [P, TOPK, UT, E], F32)
        mask_b = sb("mask_b", [P, UT, E], BF16)
        before_cnt = sb("before_cnt", [P, GUNITS + 1, E], BF16)
        unit_cnt = sb("unit_cnt", [P, E], F32)
        one_sb = sb("one_sb", [P, 1], F32)
        gap = sb("gap", [P, 3, UT], F32)
        place = sb("place", [P, UT, E], F32)
        picked = sb("picked", [P, TOPK, UT, E], F32)
        place_f = sb("place_f", [P, TOPK, UT], F32)
        iota_e = sb("iota_e", [P, E], F32)
        iota_p = sb("iota_p", [P, E], F32)
        weight_sb = sb("weight_sb", [P, TOKENS // P, TOPK], F32)
        place_i = sb("place_i", [P, TOKENS // P, TOPK], I32)
        expert_sb = sb("expert_sb", [P, TOKENS // P, TOPK], F32)
        pad_f = sb("pad_f", [P, E], F32)
        pad_i = sb("pad_i", [P, GROUPS, E], I32)
        cnt_sb = sb("cnt_sb", [P, GROUPS, E], F32)
        table_i = sb("table_i", [P, GROUPS, 2, KT], I32)
        region_row = sb("region_row", [P, GROUPS, E], F32)
        TAB = GTILES * (1 + TOPK) + 4 * E + KT * (4 + 2 * E)
        tab = sb("tab", [P, TAB], F32)

        XS, YB, PICKS = 8, 4, NSLOTS // TOPK
        ek_b = ek_odd[:, :].bitcast(BF16)
        xs_sb = ek_b[:, 0:XS * D].rearrange("p (s c t) -> p s c t", s=XS, c=J)
        y_sb = ek_b[:, XS * D:(XS + YB) * D].rearrange("p (s d) -> p s d", s=YB)
        num_b = num_sb[:, :, :].rearrange("p a b -> p (a b)").bitcast(BF16)
        silu_sb, h_sb, ht_sb = (num_b[:, i * 2 * FF:(i + 1) * 2 * FF].rearrange("p (s f) -> p s f", s=2)
                                for i in (2, 3, 4))
        pick_sb = xn_sb.rearrange("p (s k) d -> p s k d", k=TOPK)
        scan_f = scan_sb[:, :, :, :].rearrange("p a b c -> p (a b c)")
        res_slots = [ek_odd[:, (XS + YB) * D // 2 + i * D:(XS + YB) * D // 2 + (i + 1) * D] for i in range(2)]
        res_slots += [scan_f[:, 0:D], scan_f[:, D:2 * D], x1t_sb[:, :, :].rearrange("p a b -> p (a b)"),
                      den_sb[:, 0:2, :].rearrange("p a b -> p (a b)")]
        CB = len(res_slots)

        bank = [stack.enter_context(nc.psum_tensor(f"bank{i}", [P, 512], F32)) for i in range(8)]
        ps_e, ps_b, ps_x, ps_v, ps_score, ps_small = bank[0], bank[1], bank[2:4], bank[4:6], bank[6], bank[7]

        s_const, s_setup_dma, s_setup_pe, s_setup_dve, s_setup_act = map(
            sig, ("s_const", "s_setup_dma", "s_setup_pe", "s_setup_dve", "s_setup_act"))
        s_x = [sig(f"s_x_in{i}") for i in range(XSLOTS)]
        s_v = [sig(f"s_v_in{i}") for i in range(2 * UT)]
        s_spill = [sig(f"s_spill{i}") for i in range(2)]
        s_stats, s_norm1, s_nmr1, s_exp, s_ev, s_ev_dve = map(
            sig, ("s_stats", "s_norm1", "s_nmr1", "s_exp", "s_ev", "s_ev_dve"))
        s_te, s_tv, s_tx, s_back = map(sig, ("s_te", "s_tv", "s_tx", "s_back"))
        s_scan, s_den, s_num, s_log, s_inv, s_y, s_x1t, s_x1 = map(
            sig, ("s_scan", "s_den", "s_num", "s_log", "s_inv", "s_y", "s_x1t", "s_x1"))
        s_sum_xy, s_x1t_act = sig("s_sum_xy"), sig("s_x1t_act")
        s_route, s_norm2, s_nmr2, s_soft, s_weight, s_xn, s_rank = map(
            sig, ("s_route", "s_norm2", "s_nmr2", "s_soft", "s_weight", "s_xn", "s_rank"))
        s_scatter = [sig(f"s_scatter{i}") for i in range(NSLOTS)]
        s_pad, s_w13 = sig("s_pad"), sig("s_w13")
        s_w2 = sig("s_w2")
        s_table, s_total = sig("s_table"), sig("s_total")
        s_xs = [sig(f"s_xs{i}") for i in range(XS)]
        s_h, s_silu, s_gate, s_ht, s_htc, s_yp, s_ya, s_yd = map(
            sig, ("s_h", "s_silu", "s_gate", "s_ht", "s_htc", "s_yp", "s_ya", "s_yd"))
        s_yout = [sig(f"s_yout{i}") for i in range(YB)]
        s_res = [sig(f"s_res{i}") for i in range(CB)]
        s_pick = [sig(f"s_pick{i}") for i in range(PICKS)]
        s_out = [sig(f"s_out{i}") for i in range(CB + 2)]
        s_sum = sig("s_sum")

        S = Streams(("sync", "gpsimd", "scalar", "vector", "tensor"))
        put, wait = S.put, S.wait

        def diagonal(tile, compare, fill):
            made = put("gpsimd", lambda g: g.memset(tile[:, :], 1.0 - fill), s_const)
            wait("gpsimd", made)
            return put("gpsimd", lambda g: g.affine_select(
                out=tile[:, :], in_=tile[:, :], compare_op=compare, fill=fill, base=0,
                pattern=[[-1, P]], channel_multiplier=1), s_const)

        put("gpsimd", lambda g: g.memset(zero_b[:, :], 0.0), s_const)
        put("gpsimd", lambda g: g.memset(eps_sb[:, :], EPS), s_const)
        put("gpsimd", lambda g: g.memset(one_sb[:, :], 1.0), s_const)
        put("gpsimd", lambda g: g.memset(ones_b[:, :], 1.0), s_const)
        put("gpsimd", lambda g: g.memset(router_t[:, :, E:R1], 1.0), s_const)
        put("gpsimd", lambda g: g.memset(before_cnt[:, 0, :], 0.0), s_const)
        ones_f = x1t_sb[:, 0, 0:P]
        put("gpsimd", lambda g: g.memset(ones_f, 1.0), s_const)
        put("gpsimd", lambda g: g.iota(iota_e[:, :], pattern=[[1, E]], base=0, channel_multiplier=0,
                                       allow_small_or_imprecise_dtypes=True), s_const)
        put("gpsimd", lambda g: g.iota(iota_p[:, :], pattern=[[REGION * P, E]], base=0, channel_multiplier=1,
                                       allow_small_or_imprecise_dtypes=True), s_const)
        diagonal(ident, ALU.not_equal, 1.0)
        diagonal(ident_b, ALU.not_equal, 1.0)
        made = put("gpsimd", lambda g: g.memset(before_b[:, :], 1.0), s_const)
        wait("gpsimd", made)
        const = put("gpsimd", lambda g: g.affine_select(
            out=before_b[:, :], in_=before_b[:, :], compare_op=ALU.is_gt, fill=0.0, base=0,
            pattern=[[1, P]], channel_multiplier=-1), s_const)

        for g in range(GROUPS):
            regions = put("gpsimd", lambda q, g=g: q.iota(
                region_row[:, g, :], pattern=[[REGION * P, E]], base=g * GREG * P, channel_multiplier=0,
                allow_small_or_imprecise_dtypes=True), s_const)
        wait("vector", regions)

        w13 = w13_sb[:, :].rearrange("p (e c f) -> p e c f", e=E, c=J)
        w2v = w2_sb[:, :].rearrange("p (e c d) -> p e c d", e=E, c=FC)

        def load_w13(e, part):
            w = (w1, w3)[part]
            return put("gpsimd", lambda g: g.dma_start(
                w13[:, e, :, part * FF:(part + 1) * FF], w[e].rearrange("(c p) f -> p c f", p=P)), s_w13, DMA)

        def load_w2(e):
            return put("gpsimd", lambda g, e=e: g.dma_start(
                w2v[:, e, :, :], w2[e].rearrange("(c p) d -> p c d", p=P)), s_w2, DMA)

        x_in, v_in, stat, nrm, nmr, e_in, ev_in = {}, {}, {}, {}, {}, {}, {}
        te, tv, tx, den, num, inv, ym, x1t, x1m, routed_pe = {}, {}, {}, {}, {}, {}, {}, {}, {}, {}
        carried, scanned, added, spilled, squared, xn_m, scattered, copied_scores, route = (
            {}, {}, {}, {}, {}, {}, {}, {}, {})
        TENSOR_ADDS = (0, 1, 2, 3, 4, 5)
        N = UNITS * J

        def load_x(t):
            wait("sync", spilled.get(t // UT - XUNITS), xn_m.get(t - XSLOTS))
            x_in[t] = put("sync", lambda s: s.dma_start(x_tile(t), x_rows[t * P:(t + 1) * P, :]),
                          s_x[t % XSLOTS], DMA)

        def load_ctx(t):
            u, i = divmod(t, UT)
            wait("sync", tv.get((u - 2) * J + J - 1))
            v_in[t] = put("sync", lambda s: s.dma_start(ek_all[u % 2][:, 1, i, :], ctx_rows[t * P:(t + 1) * P, :]),
                          s_v[t % (2 * UT)], DMA)

        def first_norm(t):
            k = t % XSLOTS
            wait("vector", x_in[t], nmr.get(t - XSLOTS), nrm.get(t - XSLOTS))
            for h in range(2):
                mark = put("vector", lambda v, h=h: v.bn_stats(stats[:, t % 2, 6 * h:6 * h + 6],
                                                               x_tile(t)[:, h * 512:(h + 1) * 512]), s_stats)
            wait("vector", mark)
            stat[t] = put("vector", lambda v: v.bn_aggr(mv[:, k, :], stats[:, t % 2, :]), s_stats)

        def first_std(t):
            k = t % XSLOTS
            wait("scalar", stat[t], const, nmr.get(t - XSLOTS))
            mark = put("scalar", lambda a: a.activation(norm1[:, k, 0:1], mv[:, k, 1:2], ACT.Ln,
                                                        bias=eps_sb[:, 0:1]), s_norm1)
            wait("scalar", mark)
            nrm[t] = put("scalar", lambda a: a.activation(norm1[:, k, 1:2], norm1[:, k, 0:1], ACT.Exp,
                                                          scale=-0.5), s_norm1)
            wait("gpsimd", nrm[t], e_in.get((t - XSLOTS, 1)))
            nmr[t] = put("gpsimd", lambda g: g.tensor_scalar(norm1[:, k, 2:3], mv[:, k, 0:1], norm1[:, k, 1:2],
                                                             -1.0, ALU.mult, ALU.mult), s_nmr1)

        def half(h):
            return slice(h * D // 2, (h + 1) * D // 2)

        def exponential(t, h):
            u, i, k = t // UT, t % UT, t % XSLOTS
            wait("scalar", nmr[t], tv.get((u - 2) * J + J - 1))
            e_in[t, h] = put("scalar", lambda a: a.activation(
                ek_all[u % 2][:, 0, i, half(h)], x_tile(t)[:, half(h)], ACT.Exp,
                bias=norm1[:, k, 2:3], scale=norm1[:, k, 1:2]), s_exp)

        def weigh_ctx(t, h, engine="gpsimd", signal=s_ev):
            u, i = divmod(t, UT)
            wait(engine, e_in[t, h], v_in[t])
            buf = ek_all[u % 2]
            ev_in[t, h] = put(engine, lambda g: g.tensor_tensor(
                buf[:, 1, i, half(h)], buf[:, 0, i, half(h)], buf[:, 1, i, half(h)], ALU.mult), signal)

        def turn(n):
            u, j = divmod(n, J)
            buf = ek_all[u % 2]
            for part, (dst, marks, free, done, s) in enumerate((
                    (ps_e, e_in, den.get(n - 1), te, s_te), (ps_v[n % 2], ev_in, num.get(n - 2), tv, s_tv))):
                wait("tensor", const, free)
                if j % (J // 2) == 0:
                    wait("tensor", *(marks[u * UT + i, j // (J // 2)] for i in range(UT)))
                for i in range(UT):
                    done[n] = put("tensor", lambda t, i=i, dst=dst, part=part: t.transpose(
                        dst[:, i * P:(i + 1) * P], buf[:, part, i, j * P:(j + 1) * P], ident[:, :]),
                        s if i == UT - 1 else None)

        def turn_x(n):
            u, j = divmod(n, J)
            wait("tensor", x1t.get(n - 2))
            for i in range(UT):
                tx[n] = put("tensor", lambda t, i=i: t.matmul(
                    ps_x[n % 2][:, i * P:(i + 1) * P], x_unit(u)[:, i, j * P:(j + 1) * P], ident[:, :],
                    is_transpose=True, start=(i == 0), stop=(i == UT - 1 and not on_tensor(n)),
                    skip_group_check=True), s_tx if i == UT - 1 else None)

        def scan_exp(n):
            if (n // J) % PER_ROW:
                carried[n] = put("vector", lambda v: v.tensor_copy(
                    scan_sb[:, n % 2, :, 0:1], state[:, n % J, :].unsqueeze(2)), s_scan)
            scan(n, 0, ps_e, te[n])

        def scan(n, part, src, turned_m):
            j, first = n % J, (n // J) % PER_ROW == 0
            sums = scan_sb[:, n % 2, part, :]
            wait("vector", turned_m, carried.get(n))
            if first:
                put("vector", lambda v: v.tensor_copy(sums[:, 0:1], src[:, 0:1]), s_scan)
            scanned[n, part] = put("vector", lambda v: v.tensor_tensor_scan(
                out=sums[:, 1:UNIT + 1], data0=decay_k[:, j:j + 1].to_broadcast([P, UNIT]), data1=src[:, :],
                initial=0.0 if first else sums[:, 0:1], op0=ALU.mult, op1=ALU.add), s_scan)

        def add_bonus(n, part, src, dst, signal):
            j = n % J
            wait("vector", scanned[n, part])
            return put("vector", lambda v: v.scalar_tensor_tensor(
                out=dst[:, n % ND, :], in0=src[:, :], scalar=bonus_k[:, j:j + 1],
                in1=scan_sb[:, n % 2, part, 0:UNIT], op0=ALU.mult, op1=ALU.add), signal)

        def make_den(n):
            scan(n, 1, ps_v[n % 2], tv[n])
            wait("vector", ym.get(n - ND))
            den[n] = add_bonus(n, 0, ps_e, den_sb, s_den)

        def make_num(n):
            wait("vector", added.get(n - ND))
            num[n] = add_bonus(n, 1, ps_v[n % 2], num_sb, s_num)
            if (n // J) % PER_ROW < PER_ROW - 1:
                put("vector", lambda v: v.tensor_copy(
                    state[:, n % J, :].unsqueeze(2), scan_sb[:, n % 2, :, UNIT:UNIT + 1]), s_scan)

        def divide(n):
            j = n % J
            wait("scalar", den[n])
            mark = put("scalar", lambda a: a.activation(den_sb[:, n % ND, :], den_sb[:, n % ND, :], ACT.Ln,
                                                        scale=scale_k[:, j:j + 1]), s_log)
            wait("scalar", mark)
            inv[n] = put("scalar", lambda a: a.activation(den_sb[:, n % ND, :], den_sb[:, n % ND, :], ACT.Exp,
                                                          bias=shift_k[:, j:j + 1], scale=-1.0), s_inv)

        def quotient(n):
            wait("gpsimd", inv[n], num[n])
            ym[n] = put("gpsimd", lambda g: g.tensor_tensor(num_sb[:, n % ND, :], num_sb[:, n % ND, :],
                                                            den_sb[:, n % ND, :], ALU.mult), s_y)

        def on_tensor(n):
            return (n + 2) % J in TENSOR_ADDS and n < N - 2

        def add_residual(n):
            wait("vector", tx[n], ym[n], routed_pe.get(n - 2), router_summed, summed)
            x1t[n] = added[n] = put("vector", lambda v: v.tensor_tensor(
                x1t_sb[:, n % 2, :], ps_x[n % 2][:, :], num_sb[:, n % ND, :], ALU.add), s_x1t)

        def accumulate(n):
            wait("tensor", ym[n])
            added[n] = put("tensor", lambda t: t.matmul(
                ps_x[n % 2][:, :], ident[:, :], num_sb[:, n % ND, :], start=False, stop=True,
                skip_group_check=True), s_sum_xy)

        def keep_sum(n):
            wait("scalar", added[n], routed_pe.get(n - 2), summed)
            x1t[n] = put("scalar", lambda a: a.activation(x1t_sb[:, n % 2, :], ps_x[n % 2][:, :], ACT.Copy),
                         s_x1t_act)

        def turn_back(n):
            u, j = divmod(n, J)
            wait("tensor", x1t[n], x1m.get(n - 1))
            if j == 0:
                wait("tensor", copied_scores.get(u - 1))
            for i in range(UT):
                put("tensor", lambda t, i=i: t.matmul(
                    ps_score[:, i * R1:(i + 1) * R1], x1t_sb[:, n % 2, i * P:(i + 1) * P],
                    router_t[:, j, :], start=(j == 0 and i == 0), stop=(j == J - 1), skip_group_check=True))
            for i in range(UT):
                routed_pe[n] = put("tensor", lambda t, i=i: t.transpose(
                    ps_b[:, i * P:(i + 1) * P], x1t_sb[:, n % 2, i * P:(i + 1) * P], ident[:, :]),
                    s_back if i == UT - 1 else None)

        def keep_x1(n):
            u, j = divmod(n, J)
            wait("scalar", routed_pe[n])
            x1m[n] = put("scalar", lambda a: a.activation(
                x_unit(u)[:, :, j * P:(j + 1) * P],
                ps_b[:, :].rearrange("p (i c) -> p i c", i=UT), ACT.Copy), s_x1)

        def spill(u):
            wait("sync", x1m[u * J + J - 1])
            spilled[u] = put("sync", lambda s: s.dma_start(
                residual[u * UNIT:(u + 1) * UNIT, :].rearrange("(i p) d -> p i d", p=P), x_unit(u)),
                s_spill[u % 2], DMA)

        def second_mean(u):
            wait("vector", routed_pe[u * J + J - 1], xn_m.get((u - 1) * UT + UT - 1))
            copied_scores[u] = put("vector", lambda v: v.tensor_copy(
                sc_sb[:, :, :], ps_score[:, 0:UT * R1].rearrange("p (i e) -> p i e", i=UT)), s_route)
            wait("vector", copied_scores[u])
            route["mean", u] = put("vector", lambda v: v.tensor_scalar(negmean[:, :], sc_sb[:, :, E], -1.0 / D,
                                                                       None, ALU.mult), s_route)

        def square(t):
            u, i = divmod(t, UT)
            wait("scalar", x1m[u * J + J - 1], route["mean", u], scattered.get(t - NSLOTS))
            squared[t] = put("scalar", lambda a: a.activation(
                xn_sb[:, t % NSLOTS, :], x_tile(t), ACT.Square, bias=negmean[:, i:i + 1],
                accum_out=sumsq[:, i:i + 1]), s_norm2)

        def second_std(u):
            wait("scalar", squared[u * UT + UT - 1], route.get(("soft", u - 1)))
            if u == UNITS - 1:
                put("scalar", lambda a: a.preload_act_table_set("natural_log_exp_and_others"))
            mark = put("scalar", lambda a: a.activation(norm2[:, 0, :], sumsq[:, :], ACT.Ln, scale=1.0 / D,
                                                        bias=eps_sb[:, 0:1]), s_norm2)
            wait("scalar", mark)
            route["std", u] = put("scalar", lambda a: a.activation(norm2[:, 1, :], norm2[:, 0, :], ACT.Exp,
                                                                   scale=-0.5), s_norm2)
            wait("gpsimd", route["std", u])
            route["nmr", u] = put("gpsimd", lambda g: g.tensor_tensor(norm2[:, 2, :], negmean[:, :], norm2[:, 1, :],
                                                                      ALU.mult), s_nmr2)

        def best_two(u):
            wait("vector", route["mean", u], route.get(("gap", u - 1)))
            for i in range(UT):
                mark = put("vector", lambda v, i=i: v.scalar_tensor_tensor(
                    out=score[:, i, :], in0=router_sum[:, :], scalar=negmean[:, i:i + 1],
                    in1=sc_sb[:, i, 0:E], op0=ALU.mult, op1=ALU.add), s_route)
            wait("vector", mark)
            for i in range(UT):
                mark = put("vector", lambda v, i=i: v.max(top[:, i, :], score[:, i, :]), s_route)
            wait("vector", mark)
            for i in range(UT):
                mark = put("vector", lambda v, i=i: v.max_index(top_i[:, i, :], top[:, i, :], score[:, i, :]),
                           s_route)
            route["best", u] = mark

        def choices(u):
            wait("vector", route["best", u])
            mark = put("vector", lambda v: v.tensor_copy(
                top_f[:, :, :], top_i[:, :, 0:TOPK].rearrange("p i k -> p k i")), s_route)
            wait("vector", mark)
            put("vector", lambda v: v.tensor_copy(
                expert_sb[:, u * UT:(u + 1) * UT, :], top_f[:, :, :].rearrange("p k i -> p i k")), s_route)
            for k in range(TOPK):
                mark = put("vector", lambda v, k=k: v.tensor_tensor(
                    chosen[:, k, :, :], iota_e[:, :].unsqueeze(1).to_broadcast([P, UT, E]),
                    top_f[:, k, :].unsqueeze(2).to_broadcast([P, UT, E]), ALU.is_equal), s_route)
            wait("vector", mark, route.get(("rank", u - 1)))
            mark = put("vector", lambda v: v.tensor_tensor(mask_b[:, :, :], chosen[:, 0, :, :], chosen[:, 1, :, :],
                                                           ALU.add), s_route)
            g = u % GUNITS
            wait("vector", mark, route.get(("total", u // GUNITS - 1)) if g == 0 else None)
            mark = put("vector", lambda v: v.tensor_reduce(
                unit_cnt[:, :], mask_b[:, :, :].rearrange("p i e -> p e i"), AX_X, ALU.add), s_route)
            wait("vector", mark)
            mark = put("vector", lambda v: v.tensor_tensor(
                before_cnt[:, g + 1, :], before_cnt[:, g, :], unit_cnt[:, :], ALU.add), s_route)
            route["mask", u] = mark

        def rank_tokens(u):
            wait("tensor", route["mask", u], route.get(("place", u - 1)), router_summed,
                 route.get(("counted", u // GUNITS - 1)))
            for i in range(UT):
                dst = ps_small[:, i * E:(i + 1) * E]
                put("tensor", lambda t, i=i, dst=dst: t.matmul(dst, before_b[:, :], mask_b[:, i, :],
                                                               start=True, stop=False, skip_group_check=True))
                for earlier in range(i):
                    put("tensor", lambda t, earlier=earlier, dst=dst: t.matmul(
                        dst, ones_b[:, :], mask_b[:, earlier, :], start=False, stop=False, skip_group_check=True))
                route["rank", u] = put("tensor", lambda t, dst=dst: t.matmul(
                    dst, ones_b[:, :], before_cnt[:, u % GUNITS, :], start=False, stop=True,
                    skip_group_check=True), s_rank)

        def normed_row(t):
            u, i = divmod(t, UT)
            wait("scalar", route["nmr", u], squared[t])
            xn_m[t] = put("scalar", lambda a: a.activation(
                xn_sb[:, t % NSLOTS, :], x_tile(t), ACT.Identity, bias=norm2[:, 2, i:i + 1],
                scale=norm2[:, 1, i:i + 1]), s_xn)

        def score_gap(u):
            wait("gpsimd", route["std", u], route["best", u])
            mark = put("gpsimd", lambda g: g.tensor_tensor(gap[:, 0, :], top[:, :, 1], top[:, :, 0], ALU.subtract),
                       s_soft)
            wait("gpsimd", mark)
            route["gap", u] = put("gpsimd", lambda g: g.tensor_tensor(gap[:, 0, :], gap[:, 0, :], norm2[:, 1, :],
                                                                      ALU.mult), s_soft)

        def weights(u):
            t0 = u * UT
            wait("scalar", route["gap", u])
            mark = put("scalar", lambda a: a.activation(gap[:, 1, :], gap[:, 0, :], ACT.Exp), s_weight)
            wait("scalar", mark)
            mark = put("scalar", lambda a: a.activation(gap[:, 2, :], gap[:, 1, :], ACT.Ln, bias=one_sb[:, 0:1]),
                       s_weight)
            wait("scalar", mark)
            mark = put("scalar", lambda a: a.activation(weight_sb[:, t0:t0 + UT, 0], gap[:, 2, :], ACT.Exp,
                                                        scale=-1.0), s_weight)
            wait("gpsimd", mark)
            route["soft", u] = put("gpsimd", lambda g: g.tensor_tensor(
                weight_sb[:, t0:t0 + UT, 1], weight_sb[:, t0:t0 + UT, 0], gap[:, 1, :], ALU.mult), s_soft)

        def places(u):
            g, t0 = u // GUNITS, u * UT
            wait("vector", route["rank", u])
            mark = put("vector", lambda v: v.tensor_tensor(
                place[:, :, :], ps_small[:, 0:UT * E].rearrange("p (i e) -> p i e", i=UT),
                region_row[:, g, :].unsqueeze(1).to_broadcast([P, UT, E]), ALU.add), s_route)
            route["place", u] = mark
            wait("vector", mark)
            for k in range(TOPK):
                mark = put("vector", lambda v, k=k: v.tensor_tensor(
                    picked[:, k, :, :], chosen[:, k, :, :], place[:, :, :], ALU.mult), s_route)
            wait("vector", mark)
            mark = put("vector", lambda v: v.tensor_reduce(
                place_f[:, :, :], picked[:, :, :, :].rearrange("p k i e -> p (k i) e"), AX_X, ALU.add), s_route)
            wait("vector", mark)
            route["rows", u] = put("vector", lambda v: v.tensor_copy(
                place_i[:, t0:t0 + UT, :], place_f[:, :, :].rearrange("p k i -> p i k")), s_route)

        def scatter(t, k):
            wait("gpsimd", route["rows", t // UT], xn_m[t])
            scattered[t] = put("gpsimd", lambda q: q.indirect_dma_start(
                out=sorted_x, out_offset=bass.IndirectOffsetOnAxis(ap=place_i[:, t, k:k + 1], axis=0),
                in_=xn_sb[:, t % NSLOTS, :], in_offset=None), s_scatter[t % NSLOTS], DMA)

        def count_group(g):
            u = (g + 1) * GUNITS - 1
            wait("tensor", route["place", u], route["mask", u])
            route["total", g] = put("tensor", lambda t: t.matmul(
                ps_small[:, 0:E], ones_b[:, :], before_cnt[:, GUNITS, :], start=True, stop=True), s_total)

        def pad_rows(g):
            wait("vector", route["total", g])
            route["counted", g] = put("vector", lambda v: v.tensor_copy(cnt_sb[:, g, :], ps_small[:, 0:E]), s_table)
            wait("vector", route["counted", g])
            mark = put("vector", lambda v: v.scalar_tensor_tensor(
                out=pad_f[:, :], in0=cnt_sb[:, g, :], scalar=float(g * GREG * P), in1=iota_p[:, :],
                op0=ALU.add, op1=ALU.add), s_table)
            wait("vector", mark)
            route["pad rows", g] = put("vector", lambda v: v.tensor_copy(pad_i[:, g, :], pad_f[:, :]), s_table)

        def pad_expert(g, e):
            wait("gpsimd", route["pad rows", g])
            route["pad", g] = put("gpsimd", lambda q: q.indirect_dma_start(
                out=sorted_x, out_offset=bass.IndirectOffsetOnAxis(ap=pad_i[:, g, e:e + 1], axis=0),
                in_=zero_b[:, :], in_offset=None), s_pad, DMA)

        def group_scattered(g):
            last = (g + 1) * GTILES
            return [scattered[t] for t in range(last - NSLOTS, last)]

        def table_steps(g):
            M = REGION - 1
            o = [0]

            def space(shape):
                size = 1
                for s in shape:
                    size *= s
                a = tab[:, o[0]:o[0] + size]
                o[0] += size
                return a.rearrange("p (a b) -> p a b", b=shape[-1]) if len(shape) > 1 else a

            C = GTILES * TOPK
            steps, tiles, upto, one, kk, past, row, exp_, used, move, shift, products = (
                space((M,)), space((E,)), space((E,)), space((E,)), space((KT,)), space((KT, E)), space((KT,)),
                space((KT,)), space((KT,)), space((E,)), space((C,)), space((KT * E,)))
            over, same, prod = (products[:, 0:n * m].rearrange("p (a b) -> p a b", b=m)
                                for n, m in ((E, M), (C, E), (KT, E)))
            assert o[0] <= TAB
            made = []

            def constants():
                wait("gpsimd", route.get(("table", g - 1)), route["counted", g])
                put("gpsimd", lambda q: q.iota(steps, pattern=[[P, M]], base=0, channel_multiplier=0,
                                               allow_small_or_imprecise_dtypes=True), s_const)
                put("gpsimd", lambda q: q.memset(one, 1.0), s_const)
                made.append(put("gpsimd", lambda q: q.iota(kk, pattern=[[1, KT]], base=0, channel_multiplier=0,
                                                           allow_small_or_imprecise_dtypes=True), s_const))

            rows_i = place_i[:, g * GTILES:(g + 1) * GTILES, :].rearrange("p t k -> p (t k)")
            group_experts = expert_sb[:, g * GTILES:(g + 1) * GTILES, :].rearrange("p t k -> p (t k)")
            arithmetic = [
                lambda v: v.tensor_tensor(over, cnt_sb[:, g, :].unsqueeze(2).to_broadcast([P, E, M]),
                                          steps.unsqueeze(1).to_broadcast([P, E, M]), ALU.is_gt),
                lambda v: v.tensor_reduce(tiles, over, AX_X, ALU.add),
                lambda v: v.tensor_tensor_scan(out=upto, data0=one, data1=tiles, initial=0.0,
                                               op0=ALU.mult, op1=ALU.add),
                lambda v: v.tensor_tensor(past, kk.unsqueeze(2).to_broadcast([P, KT, E]),
                                          upto.unsqueeze(1).to_broadcast([P, KT, E]), ALU.is_ge),
                lambda v: v.tensor_reduce(exp_, past, AX_X, ALU.add),
                lambda v: v.tensor_tensor(move, upto, tiles, ALU.subtract),
                lambda v: v.scalar_tensor_tensor(out=move, in0=move, scalar=float(P), in1=region_row[:, g, :],
                                                 op0=ALU.mult, op1=ALU.subtract),
                lambda v: v.tensor_tensor(same, group_experts.unsqueeze(2).to_broadcast([P, C, E]),
                                          iota_e[:, :].unsqueeze(1).to_broadcast([P, C, E]), ALU.is_equal),
                lambda v: v.tensor_tensor(same, same, move.unsqueeze(1).to_broadcast([P, C, E]), ALU.mult),
                lambda v: v.tensor_reduce(shift, same, AX_X, ALU.add),
                lambda v: v.tensor_scalar(tiles, tiles, -1.0, float(REGION), ALU.mult, ALU.add),
                lambda v: v.tensor_tensor(prod, past, tiles.unsqueeze(1).to_broadcast([P, KT, E]), ALU.mult),
                lambda v: v.tensor_reduce(row, prod, AX_X, ALU.add),
                lambda v: v.tensor_tensor(row, row, kk, ALU.add),
                lambda v: v.tensor_scalar(used, exp_, float(E), None, ALU.is_lt),
                lambda v: v.tensor_tensor(row, row, used, ALU.mult),
                lambda v: v.tensor_scalar(table_i[:, g, 0, :], row, float(P), float(g * GREG * P),
                                          ALU.mult, ALU.add),
                lambda v: v.tensor_scalar(table_i[:, g, 1, :], exp_, float(E - 1), None, ALU.min)]

            def step(fn):
                wait("vector", made[0])
                route["table", g] = put("vector", fn, s_table)
                wait("vector", route["table", g])

            def shift_rows():
                wait("vector", *group_scattered(g))
                route["shifted", g] = put("vector", lambda v: v.tensor_tensor(rows_i, rows_i, shift, ALU.add),
                                          s_table)
            return [constants] + [lambda fn=fn: step(fn) for fn in arithmetic] + [shift_rows]

        xs_in, hm, sm, gm, htm, htcm, ypm, yam, ydm, yout = {}, {}, {}, {}, {}, {}, {}, {}, {}, {}
        W13_E, W2_E = J * 2 * FF, FC * D
        KTS = KT * GROUPS
        AHEAD = XS - 2
        UP_BANKS, TURN_BANKS = (ps_e, ps_v[0]), (ps_v[1], ps_x[0])
        DOWN_BANKS = (ps_b, ps_x[1]), (ps_score, ps_small)
        ROUTED = 7

        def all_of(signal):
            return signal, signal.count

        def down_banks(k):
            return DOWN_BANKS[k % 2 if k >= ROUTED else 0]

        def row_of(engine, k):
            g, kk = divmod(k, KT)
            return engine.value_load(table_i[0:1, g, 0, kk:kk + 1], min_val=0,
                                     max_val=(GROUPS * GREG - 1) * P)

        def load_sorted(k):
            g = k // KT
            wait("sync", route["table", g], route["pad", g], *group_scattered(g), tv[N - 1], hm.get(k - XS))
            xs_in[k] = put("sync", lambda s: s.dma_start_transpose(
                out=xs_sb[:, k % XS, :, :], in_=sorted_x[bass.ds(row_of(s, k), P), :]), s_xs[k % XS], DMA)

        expert_of = {}

        def gate_up(k):
            g, kk = divmod(k, KT)
            wait("tensor", route["table", g], all_of(s_w13), xs_in[k], num[N - 1], gm.get(k - 2))
            for c in range(J):
                def go(t, c=c):
                    if c == 0:
                        expert_of[k] = t.value_load(table_i[0:1, g, 1, kk:kk + 1], min_val=0, max_val=E - 1)
                    return t.matmul(UP_BANKS[k % 2][:, :], xs_sb[:, k % XS, c, :],
                                    w13_sb[:, bass.ds(expert_of[k] * W13_E + c * 2 * FF, 2 * FF)],
                                    start=(c == 0), stop=(c == J - 1))
                hm[k] = put("tensor", go, s_h if c == J - 1 else None)

        def gate(k):
            wait("scalar", hm[k], gm.get(k - 2), added[N - 3], added[N - 2])
            sm[k] = put("scalar", lambda a: a.activation(silu_sb[:, k % 2, :], UP_BANKS[k % 2][:, 0:FF], ACT.Silu), s_silu)
            wait("vector", sm[k], htm.get(k - 2))
            gm[k] = put("vector", lambda v: v.tensor_tensor(h_sb[:, k % 2, :], silu_sb[:, k % 2, :],
                                                            UP_BANKS[k % 2][:, FF:2 * FF], ALU.mult), s_gate)

        def turn_h(k):
            wait("tensor", gm[k], htcm.get(k - 2), x1t[N - 2])
            dst = TURN_BANKS[k % 2][:, :].bitcast(BF16)
            for c in range(FC):
                htm[k] = put("tensor", lambda t, c=c: t.transpose(dst[:, c * P:(c + 1) * P],
                                                                  h_sb[:, k % 2, c * P:(c + 1) * P], ident_b[:, :]),
                             s_ht if c == FC - 1 else None)
            wait("vector", htm[k], ypm.get(k - 2))
            htcm[k] = put("vector", lambda v: v.tensor_copy(ht_sb[:, k % 2, :], dst[:, 0:FF]), s_htc)

        def down(k):
            banks, former = down_banks(k), k - 1 if k < ROUTED else k - 2
            wait("tensor", htcm[k], all_of(s_w2), x1m[N - 1], x1t[N - 1], yam.get(former), ydm.get(former))
            if k == ROUTED:
                wait("tensor", route["counted", GROUPS - 1], copied_scores[UNITS - 1])
            for half in range(2):
                for c in range(FC):
                    ypm[k] = put("tensor", lambda t, half=half, c=c: t.matmul(
                        banks[half][:, :], ht_sb[:, k % 2, c * P:(c + 1) * P],
                        w2_sb[:, bass.ds(expert_of[k] * W2_E + c * D + half * 512, 512)],
                        start=(c == 0), stop=(c == FC - 1)), s_yp if c == FC - 1 else None)
            wait("scalar", ypm[k], yout.get(k - YB))
            yam[k] = put("scalar", lambda a: a.activation(y_sb[:, k % YB, 0:512], banks[0][:, :],
                                                          ACT.Copy), s_ya)
            wait("vector", ypm[k], yout.get(k - YB))
            ydm[k] = put("vector", lambda v: v.tensor_copy(y_sb[:, k % YB, 512:D], banks[1][:, :]), s_yd)

        def store_rows(k):
            wait("sync", yam[k], ydm[k])
            yout[k] = put("sync", lambda s: s.dma_start(
                expert_y[k // KT][k % KT * P:(k % KT + 1) * P, :], y_sb[:, k % YB, :]),
                          s_yout[k % YB], DMA)

        res_in, picks, sums_m, outs = {}, {}, {}, {}
        KEPT = (UNITS - 2) * UT

        def res_slot(t):
            return res_slots[t % CB] if t < KEPT else x_tile(t)

        def load_residual(t):
            if t < KEPT:
                wait("sync", num[N - 1], ym[N - 1], routed_pe[N - 1], *spilled.values(), outs.get(t - CB))
                res_in[t] = put("sync", lambda s: s.dma_start(res_slot(t), residual[t * P:(t + 1) * P, :]),
                                s_res[t % CB], DMA)

        def pick(t):
            g = t // GTILES
            wait("gpsimd", *(yout[k] for k in range((g + 1) * KT - YB, (g + 1) * KT)), sums_m.get(t - PICKS),
                 route["shifted", g])
            if t < PICKS:
                wait("gpsimd", *group_scattered(GROUPS - 1))
            for k in range(TOPK):
                picks[t] = put("gpsimd", lambda q, k=k: q.indirect_dma_start(
                    out=pick_sb[:, t % PICKS, k, :], out_offset=None, in_=expert_y[g],
                    in_offset=bass.IndirectOffsetOnAxis(ap=place_i[:, t, k:k + 1], axis=0)), s_pick[t % PICKS], DMA)

        def add_rows(t):
            wait("vector", picks[t], res_in.get(t), route["soft", t // UT])
            if t == KEPT:
                wait("vector", *(xn_m[t] for t in range(KEPT, TOKENS // P)))
            for k in range(TOPK):
                sums_m[t] = put("vector", lambda v, k=k: v.scalar_tensor_tensor(
                    out=res_slot(t), in0=pick_sb[:, t % PICKS, k, :], scalar=weight_sb[:, t, k:k + 1],
                    in1=res_slot(t), op0=ALU.mult, op1=ALU.add), s_sum)
                wait("vector", sums_m[t])
            wait("scalar", sums_m[t])
            slot = t % CB if t < KEPT else CB + t % 2
            outs[t] = put("scalar", lambda a: a.dma_start(out_rows[t * P:(t + 1) * P, :], res_slot(t)),
                          s_out[slot], DMA)

        def expert_step(m):
            if m < KTS:
                gate_up(m)
                gate(m)
            if 0 <= m - 1 < KTS:
                turn_h(m - 1)
            if 0 <= m - 2 < KTS:
                down(m - 2)
                store_rows(m - 2)
            if m + AHEAD < KTS:
                load_sorted(m + AHEAD)

        dispatched = {}
        NORMED = (7, 7, 8, 9)
        SCATTERS = {j: 1 for j in range(8, 16)}
        PADS = {j: 1 for j in range(12, 12 + E)}

        def finish(u, j):
            t0 = u * UT
            if j == 4:
                if u < UNITS - 2:
                    spill(u)
                best_two(u)
            if j == 5:
                choices(u)
            if 3 <= j < 6:
                square(t0 + j - 3)
            if j == 6:
                rank_tokens(u)
                square(t0 + 3)
                second_std(u)
                score_gap(u)
            if j == (6 if u == UNITS - 1 else 7):
                weights(u)
            for i, at in enumerate(NORMED):
                if j == at:
                    normed_row(t0 + i)
            if j == 8 and u % GUNITS == GUNITS - 1:
                count_group(u // GUNITS)
            if j == 9 and u % GUNITS == GUNITS - 1:
                pad_rows(u // GUNITS)
            if j == 7:
                places(u)
            for _ in range(SCATTERS.get(j, 0)):
                i, k = divmod(dispatched.setdefault(("scatters", u), 0), TOPK)
                scatter(t0 + i, k)
                dispatched["scatters", u] += 1
            if u % GUNITS == GUNITS - 1:
                for _ in range(PADS.get(j, 0)):
                    pad_expert(u // GUNITS, dispatched.setdefault(("pads", u), 0))
                    dispatched["pads", u] += 1

        EXPONENTIALS = (1, 2, 3, 4), (5, 6, 7, 8)

        def prepare(u, j):
            t0 = u * UT
            if j < UT:
                first_norm(t0 + j)
                first_std(t0 + j)
            for h in range(2):
                for i in range(UT):
                    if j == EXPONENTIALS[h][i]:
                        exponential(t0 + i, h)
                    if j == EXPONENTIALS[h][i] + 1:
                        weigh_ctx(t0 + i, h)

        put("scalar", lambda a: a.preload_act_table_set("natural_log_exp_and_others"))
        rows = den_sb[0:2 * J, 0, 0:P]
        router_rows = num_sb[0:E, 0:2, :].rearrange("p a b -> p (a b)")
        put("scalar", lambda a: a.dma_start(den_sb[0:J, 0, 0:P], decay.rearrange("(j p) -> j p", p=P)),
            s_setup_dma, DMA)
        put("scalar", lambda a: a.dma_start(den_sb[J:2 * J, 0, 0:P], bonus.rearrange("(j p) -> j p", p=P)),
            s_setup_dma, DMA)
        small_in = put("scalar", lambda a: a.dma_start(router_rows, router[:, :]), s_setup_dma, DMA)
        for t in range(UT):
            load_x(t)
        for t in range(UT):
            load_ctx(t)
        for t in range(UT, 2 * UT):
            load_x(t)
        for t in range(UT, 2 * UT):
            load_ctx(t)
        for t in range(2 * UT, 3 * UT):
            load_x(t)
        for t in range(UT):
            first_norm(t)
            first_std(t)
            exponential(t, 0)
        wait("tensor", const, small_in)
        for j in range(J):
            put("tensor", lambda t, j=j: t.transpose(ps_small[:, j * E:(j + 1) * E],
                                                     router_rows[:, j * P:(j + 1) * P], ident[0:E, 0:E]))
        turned = put("tensor", lambda t: t.transpose(ps_b[:, 0:2 * J], rows, ident[0:2 * J, 0:2 * J]),
                     s_setup_pe)
        wait("vector", const, turned)
        router_in = put("vector", lambda v: v.tensor_copy(
            router_t[:, :, 0:E], ps_small[:, 0:J * E].rearrange("p (j e) -> p j e", j=J)), s_setup_dve)
        put("vector", lambda v: v.tensor_copy(
            chan[:, :, :], ps_b[:, 0:2 * J].rearrange("p (s j) -> p s j", s=2)), s_setup_dve)
        wait("vector", (s_setup_dve, s_setup_dve.count))
        capped = put("vector", lambda v: v.tensor_scalar(chan_k[:, 1, :], chan[:, 1, :], U_CAP, None, ALU.min),
                     s_setup_dve)
        wait("vector", capped)
        chan_in = put("vector", lambda v: v.tensor_scalar(chan_k[:, 2, :], chan_k[:, 1, :], 0.0, -1.0, ALU.max,
                                                          ALU.mult), s_setup_dve)
        wait("scalar", chan_in)
        put("scalar", lambda a: a.activation(chan_k[:, 0, :], chan[:, 0, :], ACT.Exp), s_setup_act)
        put("scalar", lambda a: a.activation(chan_k[:, 1, :], chan_k[:, 1, :], ACT.Exp), s_setup_act)
        chan_ready = put("scalar", lambda a: a.activation(chan_k[:, 3, :], chan_k[:, 2, :], ACT.Exp), s_setup_act)
        decay_k, bonus_k, shift_k, scale_k = (chan_k[:, n, :] for n in range(4))
        wait("tensor", router_in)
        for j in range(J):
            summed = put("tensor", lambda t, j=j: t.matmul(ps_small[:, 0:E], ones_f, router_t[:, j, 0:E],
                                                           start=(j == 0), stop=(j == J - 1)),
                         s_setup_pe if j == J - 1 else None)
        for h in range(2):
            for t in range(UT):
                if h:
                    exponential(t, h)
                if t % 2 == 0 or h:
                    weigh_ctx(t, h)
                else:
                    weigh_ctx(t, h, "vector", s_ev_dve)
        wait("vector", summed)
        router_summed = put("vector", lambda v: v.tensor_copy(router_sum[:, :], ps_small[:, 0:E]), s_setup_dve)
        wait("vector", chan_ready)
        late = [(e, part) for e in range(E - LATE) for part in range(2)]
        table = []
        last_weights = [lambda e=e: load_w2(e) for e in range(3)]
        last_weights += [lambda e=e, part=part: load_w13(e, part) for e in range(E - LATE, E) for part in range(2)]
        last_weights += [lambda e=e: load_w2(e) for e in range(3, E)]
        LATE_LOADS = (1, 1, 2, 2, 2, 2, 1, 1)
        FLUSH = 4
        for n in range(N + FLUSH):
            u, j = divmod(n, J)
            if n < N:
                turn(n)
                scan_exp(n)
            if u >= 1 and j == 3:
                second_mean(u - 1)
            if 0 <= n - 1 < N:
                quotient(n - 1)
            if 0 <= n - 2 < N:
                accumulate(n - 2) if on_tensor(n - 2) else add_residual(n - 2)
            if 0 <= n - 1 < N:
                turn_x(n - 1)
            if 0 <= n - 4 < N:
                keep_x1(n - 4)
            if 0 <= n - 3 < N:
                turn_back(n - 3)
            if n < N:
                make_den(n)
            for age in range(1, 4):
                if u >= age:
                    finish(u - age, j + (age - 1) * J)
            if u + 1 < UNITS:
                prepare(u + 1, j)
            if 1 <= u < UNITS:
                prepare(u, j + J)
            if 0 <= n - 2 < N and on_tensor(n - 2):
                keep_sum(n - 2)
            if n < N:
                make_num(n)
                divide(n)
            for i, at in enumerate(NORMED):
                v = u + 2 - at // J
                if j == at % J and 3 <= v < UNITS:
                    load_x(v * UT + i)
            if j == 1 and 2 <= u + 1 < UNITS:
                for i in range(UT):
                    load_ctx((u + 1) * UT + i)
            if late and n >= 2:
                load_w13(*late.pop(0))
            if u == UNITS - 1:
                wait("gpsimd", tv[u * J - 1])
                if j >= 2:
                    wait("gpsimd", xn_m[(UNITS - 2) * UT - 1], spilled[UNITS - 3])
                for _ in range(LATE_LOADS[j]):
                    last_weights.pop(0)()
            if n == (GUNITS + 1) * J + 2:
                table = table_steps(0)
            if table:
                table.pop(0)()
            if n == N:
                for k in range(AHEAD):
                    load_sorted(k)
            if n in (N, N + 1):
                gate_up(n - N)
                load_sorted(n - N + AHEAD)
            if n == N + 2:
                gate(0)
                gate(1)
                turn_h(0)
            if n == N + FLUSH - 1:
                expert_step(2)

        for m in range(FLUSH - 1, KTS + 3):
            finish(UNITS - 2, m + 1 + J)
            finish(UNITS - 1, m + 1)
            if m == KT // 2:
                table = table_steps(GROUPS - 1)
            if table:
                table.pop(0)()
                table.pop(0)() if table else None
            expert_step(m)
            if m == KT // 2:
                for t in range(CB):
                    load_residual(t)
            c, odd = divmod(m - KT - 3, 2)
            if c >= 0 and not odd and c < GTILES:
                pick(c)
            if c >= 1 and odd and c - 1 < GTILES:
                add_rows(c - 1)
                load_residual(c - 1 + CB)
        for t in range(GTILES, TOKENS // P):
            pick(t)
            if t > GTILES:
                add_rows(t - 1)
                load_residual(t - 1 + CB)
        add_rows(TOKENS // P - 1)
        for s in (*s_out, *s_yout, *s_spill, *s_scatter, s_pad):
            wait("sync", (s, s.count))

        block = stack.enter_context(nc.Block())
        block.sync(lambda e: S.emit("sync", e))
        block.gpsimd(lambda e: S.emit("gpsimd", e))
        block.scalar(lambda e: S.emit("scalar", e))
        block.vector(lambda e: S.emit("vector", e))
        block.tensor(lambda e: S.emit("tensor", e))


_INS = ['x', 'ctx_2048', 'L0_xattn_w', 'L0_xattn_u', 'L0_ffn_router_w', 'L0_ffn_w1', 'L0_ffn_w2', 'L0_ffn_w3']


def kernel(**inputs):
    import numpy as _np
    import concourse.bacc as _bacc
    from concourse import mybir as _mybir
    from concourse.bass_utils import run_bass_kernel_spmd as _run

    nc = _bacc.Bacc("TRN2", target_bir_lowering=False, num_devices=1)
    arrays, args = {}, []
    for name in _INS:
        a = _np.ascontiguousarray(inputs[name])
        arrays[f"in_{name}_dram"] = a
        args.append(nc.dram_tensor(f"in_{name}_dram", a.shape, _mybir.dt.from_np(a.dtype), kind="ExternalInput").ap())
    out = nc.dram_tensor("out_0_dram", inputs['x'].shape, _mybir.dt.float32, kind="ExternalOutput").ap()
    wkv_moe(nc, *args, out)
    r = _run(nc, [arrays], core_ids=[0])
    return r.results[0]["out_0_dram"]
```
